# Optimizing a Trainium2 kernel written in Bass

```python
import numpy as np
import jax
import jax.numpy as jnp

def _softmax(x, axis=-1):
    return jax.nn.softmax(x, axis=axis)

def _gelu(x):
    return jax.nn.gelu(x, approximate=True)

def _silu(x):
    return jax.nn.silu(x)

def _sigmoid(x):
    return jax.nn.sigmoid(x)

def _layernorm(x, axis=-1, eps=1e-05):
    m = jnp.mean(x, axis=axis, keepdims=True)
    v = jnp.var(x, axis=axis, keepdims=True)
    return (x - m) / jnp.sqrt(v + eps)

def _scatter_add(tgt, idx, src, axis=0):
    return tgt.at[idx].add(src)

def _segment_sum(src, seg, n):
    return jax.ops.segment_sum(src, seg, n)
kernel_name = 'mk_xattn_ffn_d2_seqx_r8_2829e3'

def setup_inputs(seed: int=0):
    np.random.seed(seed)
    _w = jnp.asarray

    def _rec_inputs():
        import jax
        import jax.numpy as jnp
        _rk = jax.random.key(seed)
        x = -0.0002928 + 1 * jax.random.normal(jax.random.fold_in(_rk, 1), (8, 256, 128), jnp.float32)
        _lenS = 256 - jax.random.randint(jax.random.fold_in(_rk, 7), (8,), 0, max(1, 256 // 4) + 1, jnp.int32)
        _lenS2 = 256 - jax.random.randint(jax.random.fold_in(_rk, 8), (8,), 0, max(1, 256 // 4) + 1, jnp.int32)
        _ctx_1024P = jax.random.normal(jax.random.fold_in(_rk, 11), (8, 16, 128), jnp.float32)
        _ctx_1024c = jax.random.dirichlet(jax.random.fold_in(_rk, 511), 0.3 * jnp.ones((16,), jnp.float32), (8, 256))
        _ctx_1024t = jnp.einsum('bsk,bkd->bsd', _ctx_1024c, _ctx_1024P)
        _ctx_1024t = _ctx_1024t * jax.lax.rsqrt(jnp.mean(jnp.square(_ctx_1024t)) + 1e-12) * 0.953939
        ctx_1024 = -1.39393e-06 + 0.999914 * (_ctx_1024t + 0.3 * jax.random.normal(jax.random.fold_in(_rk, 611), (8, 256, 128), jnp.float32))
        _validS = jnp.arange(256)[None, :] < _lenS[:, None]
        _validS2 = jnp.arange(256)[None, :] < _lenS2[:, None]
        _causal = jnp.tril(jnp.ones((256, 256), dtype=bool))
        mask_Bx1xSxS2_ik0 = jnp.where(jnp.broadcast_to(_validS2[:, None, None, :], (8, 1, 256, 256)), 0, 1).astype(jnp.int32)
        mask_Bx1xSxS2_if1 = jnp.where(jnp.ones((8, 1, 256, 256), dtype=bool), 1, 0).astype(jnp.int32)
        return (x, ctx_1024, mask_Bx1xSxS2_ik0, mask_Bx1xSxS2_if1)
    x, ctx_1024, mask_Bx1xSxS2_ik0, mask_Bx1xSxS2_if1 = _rec_inputs()

    def _L0_xattn_setup():
        import jax, jax.numpy as jnp
        import numpy as np
        import math
        D_MODEL = 128
        NUM_HEADS = 16
        MAX_LEN = 256
        D_HEAD = D_MODEL // NUM_HEADS
        BATCH = 2
        SEQ = 256

        def _skew(QEr):
            B, H, R, C = QEr.shape
            padded = jnp.pad(QEr, ((0, 0), (0, 0), (0, 0), (1, 0)))
            reshaped = padded.reshape(B, H, C + 1, R)
            return reshaped[:, :, 1:, :]
        root = jax.random.key(seed)
        ks = jax.random.split(root, 10)
        s = 1.0 / math.sqrt(D_MODEL)
        return {'query': jax.random.normal(ks[0], (BATCH, SEQ, D_MODEL), jnp.float32), 'key': jax.random.normal(ks[1], (BATCH, SEQ, D_MODEL), jnp.float32), 'value': jax.random.normal(ks[2], (BATCH, SEQ, D_MODEL), jnp.float32), 'Wq': jax.random.normal(ks[3], (D_MODEL, D_MODEL), jnp.float32) * s, 'bq': jax.random.normal(ks[4], (D_MODEL,), jnp.float32) * s, 'Wk': jax.random.normal(ks[5], (D_MODEL, D_MODEL), jnp.float32) * s, 'bk': jax.random.normal(ks[6], (D_MODEL,), jnp.float32) * s, 'Wv': jax.random.normal(ks[7], (D_MODEL, D_MODEL), jnp.float32) * s, 'bv': jax.random.normal(ks[8], (D_MODEL,), jnp.float32) * s, 'Er': jax.random.normal(ks[9], (MAX_LEN, D_HEAD), jnp.float32)}
    _L0_xattn_all = _L0_xattn_setup()
    _L0_xattn_in = {k: v for k, v in _L0_xattn_all.items() if k in ('Wq', 'bq', 'Wk', 'bk', 'Wv', 'bv', 'Er')}
    del _L0_xattn_all

    def _L0_ffn_setup():
        import jax, jax.numpy as jnp
        import numpy as np
        B, S, D, E, H = (2, 128, 128, 16, 256)
        TOP_K = 2
        TEMP = 1.0
        key = jax.random.key(seed)
        ks = jax.random.split(key, 4)
        sc_d = 1.0 / np.sqrt(D)
        sc_h = 1.0 / np.sqrt(H)
        return {'x': jax.random.normal(ks[0], (B, S, D), dtype=jnp.float32), 'Wr': jax.random.normal(ks[1], (D, E), dtype=jnp.float32) * sc_d, 'br': jnp.zeros((E,), dtype=jnp.float32), 'W1': jax.random.normal(ks[2], (E, D, H), dtype=jnp.float32) * sc_d, 'b1': jnp.zeros((E, H), dtype=jnp.float32), 'W2': jax.random.normal(ks[3], (E, H, D), dtype=jnp.float32) * sc_h, 'b2': jnp.zeros((E, D), dtype=jnp.float32)}
    _L0_ffn_all = _L0_ffn_setup()
    _L0_ffn_in = {k: v for k, v in _L0_ffn_all.items() if k in ('Wr', 'br', 'W1', 'b1', 'W2', 'b2')}
    del _L0_ffn_all

    def _L1_xattn_setup():
        import jax, jax.numpy as jnp
        import numpy as np
        import math
        D_MODEL = 128
        N_HEADS = 16
        D_FF = 512
        B = 2
        S = 256
        EPS = 1e-05

        def _layer_norm(x, g, b):
            mu = jnp.mean(x, axis=-1, keepdims=True)
            var = jnp.mean(jnp.square(x - mu), axis=-1, keepdims=True)
            return (x - mu) * jax.lax.rsqrt(var + EPS) * g + b

        def _mha(q_in, k_in, v_in, mask, Wq, bq, Wk, bk, Wv, bv, Wo, bo):
            Bsz, Sq, D = q_in.shape
            Sk = k_in.shape[1]
            dk = D // N_HEADS
            q = (q_in @ Wq + bq).reshape(Bsz, Sq, N_HEADS, dk).transpose(0, 2, 1, 3)
            k = (k_in @ Wk + bk).reshape(Bsz, Sk, N_HEADS, dk).transpose(0, 2, 1, 3)
            v = (v_in @ Wv + bv).reshape(Bsz, Sk, N_HEADS, dk).transpose(0, 2, 1, 3)
            scores = jnp.einsum('bhqd,bhkd->bhqk', q, k) / math.sqrt(dk)
            scores = jnp.where(mask == 0, jnp.float32(-1000000000.0), scores)
            attn = jax.nn.softmax(scores, axis=-1)
            ctx = jnp.einsum('bhqk,bhkd->bhqd', attn, v)
            ctx = ctx.transpose(0, 2, 1, 3).reshape(Bsz, Sq, D)
            return ctx @ Wo + bo
        key = jax.random.key(seed)
        ks = jax.random.split(key, 20)
        sc = 1.0 / math.sqrt(D_MODEL)
        d = {'tgt': jax.random.normal(ks[0], (B, S, D_MODEL), jnp.float32), 'memory': jax.random.normal(ks[1], (B, S, D_MODEL), jnp.float32), 'tgt_mask': jnp.tril(jnp.ones((S, S), jnp.int32))[None, None, :, :] * jnp.ones((B, 1, 1, 1), jnp.int32), 'memory_mask': jnp.ones((B, 1, S, S), jnp.int32)}
        names = ['sa_Wq', 'sa_Wk', 'sa_Wv', 'sa_Wo', 'ca_Wq', 'ca_Wk', 'ca_Wv', 'ca_Wo']
        for i, n in enumerate(names):
            d[n] = jax.random.normal(ks[2 + i], (D_MODEL, D_MODEL), jnp.float32) * sc
            d[n.replace('W', 'b')] = jnp.zeros((D_MODEL,), jnp.float32)
        d['ff_W1'] = jax.random.normal(ks[10], (D_MODEL, D_FF), jnp.float32) * sc
        d['ff_b1'] = jnp.zeros((D_FF,), jnp.float32)
        d['ff_W2'] = jax.random.normal(ks[11], (D_FF, D_MODEL), jnp.float32) * (1.0 / math.sqrt(D_FF))
        d['ff_b2'] = jnp.zeros((D_MODEL,), jnp.float32)
        for i in (1, 2, 3):
            d[f'ln{i}_g'] = jnp.ones((D_MODEL,), jnp.float32)
            d[f'ln{i}_b'] = jnp.zeros((D_MODEL,), jnp.float32)
        return d
    _L1_xattn_all = _L1_xattn_setup()
    _L1_xattn_in = {k: v for k, v in _L1_xattn_all.items() if k in ('sa_Wq', 'sa_bq', 'sa_Wk', 'sa_bk', 'sa_Wv', 'sa_bv', 'sa_Wo', 'sa_bo', 'ca_Wq', 'ca_bq', 'ca_Wk', 'ca_bk', 'ca_Wv', 'ca_bv', 'ca_Wo', 'ca_bo', 'ff_W1', 'ff_b1', 'ff_W2', 'ff_b2', 'ln1_g', 'ln1_b', 'ln2_g', 'ln2_b', 'ln3_g', 'ln3_b')}
    del _L1_xattn_all

    def _L1_ffn_setup():
        import jax, jax.numpy as jnp
        import numpy as np
        E = 16
        K = 4
        NG = 4
        TG = 2
        SCALE = 2.5
        NORM_TOPK = True
        H = 128
        I = 64
        SH_I = I * 2
        B, S = (2, 256)
        key = jax.random.key(seed)
        ks = jax.random.split(key, 9)

        def w(k, shape, fan_in):
            return jax.random.normal(k, shape, jnp.float32) * (1.0 / np.sqrt(fan_in))
        return {'hidden_states': jax.random.normal(ks[0], (B, S, H), jnp.float32), 'gate_w': w(ks[1], (E, H), H), 'gate_bias': jnp.zeros((E,), jnp.float32), 'Wg': w(ks[2], (E, I, H), H), 'Wu': w(ks[3], (E, I, H), H), 'Wd': w(ks[4], (E, H, I), I), 'Ws_g': w(ks[5], (SH_I, H), H), 'Ws_u': w(ks[6], (SH_I, H), H), 'Ws_d': w(ks[7], (H, SH_I), SH_I)}
    _L1_ffn_all = _L1_ffn_setup()
    _L1_ffn_in = {k: v for k, v in _L1_ffn_all.items() if k in ('gate_w', 'gate_bias', 'Wg', 'Wu', 'Wd', 'Ws_g', 'Ws_u', 'Ws_d')}
    del _L1_ffn_all
    return {'x': x, 'ctx_1024': ctx_1024, 'mask_Bx1xSxS2_ik0': mask_Bx1xSxS2_ik0, 'mask_Bx1xSxS2_if1': mask_Bx1xSxS2_if1, 'L0_xattn_Wq': _L0_xattn_in['Wq'], 'L0_xattn_bq': _L0_xattn_in['bq'], 'L0_xattn_Wk': _L0_xattn_in['Wk'], 'L0_xattn_bk': _L0_xattn_in['bk'], 'L0_xattn_Wv': _L0_xattn_in['Wv'], 'L0_xattn_bv': _L0_xattn_in['bv'], 'L0_xattn_Er': _L0_xattn_in['Er'], 'L0_ffn_Wr': _L0_ffn_in['Wr'], 'L0_ffn_br': _L0_ffn_in['br'], 'L0_ffn_W1': _L0_ffn_in['W1'], 'L0_ffn_b1': _L0_ffn_in['b1'], 'L0_ffn_W2': _L0_ffn_in['W2'], 'L0_ffn_b2': _L0_ffn_in['b2'], 'L1_xattn_sa_Wq': _L1_xattn_in['sa_Wq'], 'L1_xattn_sa_bq': _L1_xattn_in['sa_bq'], 'L1_xattn_sa_Wk': _L1_xattn_in['sa_Wk'], 'L1_xattn_sa_bk': _L1_xattn_in['sa_bk'], 'L1_xattn_sa_Wv': _L1_xattn_in['sa_Wv'], 'L1_xattn_sa_bv': _L1_xattn_in['sa_bv'], 'L1_xattn_sa_Wo': _L1_xattn_in['sa_Wo'], 'L1_xattn_sa_bo': _L1_xattn_in['sa_bo'], 'L1_xattn_ca_Wq': _L1_xattn_in['ca_Wq'], 'L1_xattn_ca_bq': _L1_xattn_in['ca_bq'], 'L1_xattn_ca_Wk': _L1_xattn_in['ca_Wk'], 'L1_xattn_ca_bk': _L1_xattn_in['ca_bk'], 'L1_xattn_ca_Wv': _L1_xattn_in['ca_Wv'], 'L1_xattn_ca_bv': _L1_xattn_in['ca_bv'], 'L1_xattn_ca_Wo': _L1_xattn_in['ca_Wo'], 'L1_xattn_ca_bo': _L1_xattn_in['ca_bo'], 'L1_xattn_ff_W1': _L1_xattn_in['ff_W1'], 'L1_xattn_ff_b1': _L1_xattn_in['ff_b1'], 'L1_xattn_ff_W2': _L1_xattn_in['ff_W2'], 'L1_xattn_ff_b2': _L1_xattn_in['ff_b2'], 'L1_xattn_ln1_g': _L1_xattn_in['ln1_g'], 'L1_xattn_ln1_b': _L1_xattn_in['ln1_b'], 'L1_xattn_ln2_g': _L1_xattn_in['ln2_g'], 'L1_xattn_ln2_b': _L1_xattn_in['ln2_b'], 'L1_xattn_ln3_g': _L1_xattn_in['ln3_g'], 'L1_xattn_ln3_b': _L1_xattn_in['ln3_b'], 'L1_ffn_gate_w': _L1_ffn_in['gate_w'], 'L1_ffn_gate_bias': _L1_ffn_in['gate_bias'], 'L1_ffn_Wg': _L1_ffn_in['Wg'], 'L1_ffn_Wu': _L1_ffn_in['Wu'], 'L1_ffn_Wd': _L1_ffn_in['Wd'], 'L1_ffn_Ws_g': _L1_ffn_in['Ws_g'], 'L1_ffn_Ws_u': _L1_ffn_in['Ws_u'], 'L1_ffn_Ws_d': _L1_ffn_in['Ws_d']}

def reference(x, ctx_1024, mask_Bx1xSxS2_ik0, mask_Bx1xSxS2_if1, L0_xattn_Wq, L0_xattn_bq, L0_xattn_Wk, L0_xattn_bk, L0_xattn_Wv, L0_xattn_bv, L0_xattn_Er, L0_ffn_Wr, L0_ffn_br, L0_ffn_W1, L0_ffn_b1, L0_ffn_W2, L0_ffn_b2, L1_xattn_sa_Wq, L1_xattn_sa_bq, L1_xattn_sa_Wk, L1_xattn_sa_bk, L1_xattn_sa_Wv, L1_xattn_sa_bv, L1_xattn_sa_Wo, L1_xattn_sa_bo, L1_xattn_ca_Wq, L1_xattn_ca_bq, L1_xattn_ca_Wk, L1_xattn_ca_bk, L1_xattn_ca_Wv, L1_xattn_ca_bv, L1_xattn_ca_Wo, L1_xattn_ca_bo, L1_xattn_ff_W1, L1_xattn_ff_b1, L1_xattn_ff_W2, L1_xattn_ff_b2, L1_xattn_ln1_g, L1_xattn_ln1_b, L1_xattn_ln2_g, L1_xattn_ln2_b, L1_xattn_ln3_g, L1_xattn_ln3_b, L1_ffn_gate_w, L1_ffn_gate_bias, L1_ffn_Wg, L1_ffn_Wu, L1_ffn_Wd, L1_ffn_Ws_g, L1_ffn_Ws_u, L1_ffn_Ws_d):
    import jax
    import jax.numpy as jnp

    def _L0_xattn_ref(query, key, value, Wq, bq, Wk, bk, Wv, bv, Er):
        import jax, jax.numpy as jnp
        import numpy as np
        import math
        D_MODEL = 128
        NUM_HEADS = 16
        MAX_LEN = 256
        D_HEAD = D_MODEL // NUM_HEADS
        BATCH = 2
        SEQ = 256

        def _skew(QEr):
            B, H, R, C = QEr.shape
            padded = jnp.pad(QEr, ((0, 0), (0, 0), (0, 0), (1, 0)))
            reshaped = padded.reshape(B, H, C + 1, R)
            return reshaped[:, :, 1:, :]
        B, S, D = query.shape
        H, dh = (NUM_HEADS, D_HEAD)
        q = (jnp.einsum('bsd,ed->bse', query, Wq) + bq).reshape(B, S, H, dh).transpose(0, 2, 1, 3)
        k = (jnp.einsum('bsd,ed->bse', key, Wk) + bk).reshape(B, S, H, dh).transpose(0, 2, 1, 3)
        v = (jnp.einsum('bsd,ed->bse', value, Wv) + bv).reshape(B, S, H, dh).transpose(0, 2, 1, 3)
        start = MAX_LEN - S
        Er_s = Er[start:, :]
        QEr = jnp.einsum('bhsd,ld->bhsl', q, Er_s)
        Srel = _skew(QEr)
        QK = jnp.einsum('bhsd,bhtd->bhst', q, k)
        attn = (QK + Srel) / math.sqrt(dh)
        causal = jnp.tril(jnp.ones((S, S), dtype=bool))
        attn = jnp.where(causal[None, None], attn, -jnp.inf)
        attn = jax.nn.softmax(attn, axis=-1)
        out = jnp.einsum('bhst,bhtd->bhsd', attn, v)
        out = out.transpose(0, 2, 1, 3).reshape(B, S, D)
        return out

    def _L0_ffn_ref(x, Wr, br, W1, b1, W2, b2):
        import jax, jax.numpy as jnp
        import numpy as np
        B, S, D, E, H = (2, 128, 128, 16, 256)
        TOP_K = 2
        TEMP = 1.0
        token_shape = x.shape[:-1]
        d = x.shape[-1]
        xt = x.reshape(-1, d)
        T = xt.shape[0]
        logits = (xt @ Wr + br) / TEMP
        probs = jax.nn.softmax(logits, axis=-1)
        w, idx = jax.lax.top_k(probs, TOP_K)
        w = w / jnp.clip(jnp.sum(w, axis=-1, keepdims=True), 1e-09)
        comb = jnp.zeros((T, E), dtype=xt.dtype)
        comb = comb.at[jnp.arange(T)[:, None], idx].add(w)
        h = jax.nn.gelu(jnp.einsum('td,edh->teh', xt, W1) + b1, approximate=False)
        o = jnp.einsum('teh,eho->teo', h, W2) + b2
        y = jnp.einsum('teo,te->to', o, comb)
        y = xt + y
        return y.reshape(*token_shape, d)

    def _L1_xattn_ref(tgt, memory, tgt_mask, memory_mask, sa_Wq, sa_bq, sa_Wk, sa_bk, sa_Wv, sa_bv, sa_Wo, sa_bo, ca_Wq, ca_bq, ca_Wk, ca_bk, ca_Wv, ca_bv, ca_Wo, ca_bo, ff_W1, ff_b1, ff_W2, ff_b2, ln1_g, ln1_b, ln2_g, ln2_b, ln3_g, ln3_b):
        import jax, jax.numpy as jnp
        import numpy as np
        import math
        D_MODEL = 128
        N_HEADS = 16
        D_FF = 512
        B = 2
        S = 256
        EPS = 1e-05

        def _layer_norm(x, g, b):
            mu = jnp.mean(x, axis=-1, keepdims=True)
            var = jnp.mean(jnp.square(x - mu), axis=-1, keepdims=True)
            return (x - mu) * jax.lax.rsqrt(var + EPS) * g + b

        def _mha(q_in, k_in, v_in, mask, Wq, bq, Wk, bk, Wv, bv, Wo, bo):
            Bsz, Sq, D = q_in.shape
            Sk = k_in.shape[1]
            dk = D // N_HEADS
            q = (q_in @ Wq + bq).reshape(Bsz, Sq, N_HEADS, dk).transpose(0, 2, 1, 3)
            k = (k_in @ Wk + bk).reshape(Bsz, Sk, N_HEADS, dk).transpose(0, 2, 1, 3)
            v = (v_in @ Wv + bv).reshape(Bsz, Sk, N_HEADS, dk).transpose(0, 2, 1, 3)
            scores = jnp.einsum('bhqd,bhkd->bhqk', q, k) / math.sqrt(dk)
            scores = jnp.where(mask == 0, jnp.float32(-1000000000.0), scores)
            attn = jax.nn.softmax(scores, axis=-1)
            ctx = jnp.einsum('bhqk,bhkd->bhqd', attn, v)
            ctx = ctx.transpose(0, 2, 1, 3).reshape(Bsz, Sq, D)
            return ctx @ Wo + bo
        sa = _mha(tgt, tgt, tgt, tgt_mask, sa_Wq, sa_bq, sa_Wk, sa_bk, sa_Wv, sa_bv, sa_Wo, sa_bo)
        x = _layer_norm(tgt + sa, ln1_g, ln1_b)
        ca = _mha(x, memory, memory, memory_mask, ca_Wq, ca_bq, ca_Wk, ca_bk, ca_Wv, ca_bv, ca_Wo, ca_bo)
        x = _layer_norm(x + ca, ln2_g, ln2_b)
        ff = jax.nn.relu(x @ ff_W1 + ff_b1) @ ff_W2 + ff_b2
        return _layer_norm(x + ff, ln3_g, ln3_b)

    def _L1_ffn_ref(hidden_states, gate_w, gate_bias, Wg, Wu, Wd, Ws_g, Ws_u, Ws_d):
        import jax, jax.numpy as jnp
        import numpy as np
        E = 16
        K = 4
        NG = 4
        TG = 2
        SCALE = 2.5
        NORM_TOPK = True
        H = 128
        I = 64
        SH_I = I * 2
        B, S = (2, 256)
        x = hidden_states
        b, s, h = x.shape
        n = b * s
        xf = x.reshape(n, h)
        logits = xf @ gate_w.T
        scores = jax.nn.sigmoid(logits)
        sfc = scores + gate_bias
        epg = E // NG
        grp = sfc.reshape(n, NG, epg)
        g_scores = jax.lax.top_k(grp, 2)[0].sum(-1)
        _, gidx = jax.lax.top_k(g_scores, TG)
        gmask = jax.nn.one_hot(gidx, NG, dtype=sfc.dtype).sum(1)
        emask = jnp.repeat(gmask, epg, axis=1)
        masked = jnp.where(emask > 0, sfc, -jnp.inf)
        _, topk_idx = jax.lax.top_k(masked, K)
        topk_w = jnp.take_along_axis(scores, topk_idx, axis=1)
        if K > 1 and NORM_TOPK:
            topk_w = topk_w / (topk_w.sum(-1, keepdims=True) + 1e-20)
        topk_w = topk_w * SCALE
        cw = (jax.nn.one_hot(topk_idx, E, dtype=topk_w.dtype) * topk_w[..., None]).sum(1)
        hg = jnp.einsum('nh,eih->nei', xf, Wg)
        hu = jnp.einsum('nh,eih->nei', xf, Wu)
        act = jax.nn.silu(hg) * hu
        y = jnp.einsum('nei,ne,ehi->nh', act, cw, Wd)
        shared = jax.nn.silu(xf @ Ws_g.T) * (xf @ Ws_u.T) @ Ws_d.T
        y = y + shared
        return (x + y.reshape(b, s, h)).astype(hidden_states.dtype)
    x = x + _L0_xattn_ref(_layernorm(x, axis=-1), ctx_1024, ctx_1024, L0_xattn_Wq, L0_xattn_bq, L0_xattn_Wk, L0_xattn_bk, L0_xattn_Wv, L0_xattn_bv, L0_xattn_Er)
    x = x + _L0_ffn_ref(_layernorm(x, axis=-1), L0_ffn_Wr, L0_ffn_br, L0_ffn_W1, L0_ffn_b1, L0_ffn_W2, L0_ffn_b2)
    x = x + _L1_xattn_ref(_layernorm(x, axis=-1), ctx_1024, mask_Bx1xSxS2_ik0, mask_Bx1xSxS2_if1, L1_xattn_sa_Wq, L1_xattn_sa_bq, L1_xattn_sa_Wk, L1_xattn_sa_bk, L1_xattn_sa_Wv, L1_xattn_sa_bv, L1_xattn_sa_Wo, L1_xattn_sa_bo, L1_xattn_ca_Wq, L1_xattn_ca_bq, L1_xattn_ca_Wk, L1_xattn_ca_bk, L1_xattn_ca_Wv, L1_xattn_ca_bv, L1_xattn_ca_Wo, L1_xattn_ca_bo, L1_xattn_ff_W1, L1_xattn_ff_b1, L1_xattn_ff_W2, L1_xattn_ff_b2, L1_xattn_ln1_g, L1_xattn_ln1_b, L1_xattn_ln2_g, L1_xattn_ln2_b, L1_xattn_ln3_g, L1_xattn_ln3_b)
    x = x + _L1_ffn_ref(_layernorm(x, axis=-1), L1_ffn_gate_w, L1_ffn_gate_bias, L1_ffn_Wg, L1_ffn_Wu, L1_ffn_Wd, L1_ffn_Ws_g, L1_ffn_Ws_u, L1_ffn_Ws_d)
    return x

_drawn_inputs = setup_inputs


def setup_inputs(seed=0):
    import zlib

    import numpy as np

    out = dict(_drawn_inputs(seed))
    spreads = {'L0_ffn_br': (0.0, 0.1),
     'L0_ffn_b1': (0.0, 0.1),
     'L0_ffn_b2': (0.0, 0.1),
     'L1_xattn_sa_bq': (0.0, 0.481),
     'L1_xattn_sa_bk': (0.0, 0.8),
     'L1_xattn_sa_bv': (0.0, 0.1),
     'L1_xattn_sa_bo': (0.0, 0.1),
     'L1_xattn_ca_bq': (0.0, 0.431),
     'L1_xattn_ca_bk': (0.0, 0.8),
     'L1_xattn_ca_bv': (0.0, 0.1),
     'L1_xattn_ca_bo': (0.0, 0.1),
     'L1_xattn_ff_b1': (0.0, 0.1),
     'L1_xattn_ff_b2': (0.0, 0.1),
     'L1_xattn_ln1_g': (1.0, 0.2),
     'L1_xattn_ln1_b': (0.0, 0.1),
     'L1_xattn_ln2_g': (1.0, 0.2),
     'L1_xattn_ln2_b': (0.0, 0.1),
     'L1_xattn_ln3_g': (1.0, 0.2),
     'L1_xattn_ln3_b': (0.0, 0.1),
     'L1_ffn_gate_bias': (0.0, 0.1)}
    factors = {'L0_xattn_bk': 8.0}
    for name, (base, spread) in spreads.items():
        noise = np.random.default_rng([zlib.crc32(name.encode()), seed]).standard_normal(out[name].shape)
        drawn = base * np.exp(spread * noise) if base else spread * noise
        out[name] = jnp.asarray(drawn.astype(out[name].dtype))
    for name, factor in factors.items():
        out[name] = (out[name] * factor).astype(out[name].dtype)
    return out
```

```python
from collections import defaultdict
from contextlib import ExitStack

import concourse.bass as bass
from concourse import mybir

F32 = mybir.dt.float32
BF16 = mybir.dt.bfloat16
I32 = mybir.dt.int32
ALU = mybir.AluOpType
ACT = mybir.ActivationFunctionType
AX = mybir.AxisListType

P = 128
BATCH, SEQ = 8, 256
PAIR = 2
PASSES = BATCH // PAIR
TILES = PAIR * SEQ // P
TOK = PAIR * SEQ
HEADS, DH = 16, 8
PARTS = 3
STACK = PARTS * PARTS * DH
SCALE = DH ** -0.5
MASKED = -1e9 / SCALE
CAUSAL = -1e30
EPS = 1e-5
NEXP = 16
HID0 = 256
CH0 = NEXP * HID0 // P
CH1 = 1 + NEXP * 64 // P
CHF = 4
GROUP = 4
GROUPS = HEADS // GROUP
UNITS = HEADS * PAIR
RELW = 384
BIG = 3e38

COL_BQ, COL_BK, COL_B1, COL_FB1, COL_FB2 = 0, 3, 6, 6 + CH0, 6 + CH0 + CHF
NCOL = COL_FB2 + 1
ROW_BV, ROW_BO, ROW_G, ROW_B, ROW_R = 0, 3, 5, 8, 11
NROW = 12
W_Q, W_K, W_V, W_O = (0, 3, 7), (1, 4, 8), (2, 5, 9), (None, 6, 10)
NWA = 11


class Tally:

    def __init__(self, eng):
        self.eng, self.n = eng, defaultdict(int)

    def done(self, ins, sem):
        ins.then_inc(sem, 1)
        self.n[sem.name] += 1

    def settle(self, sem):
        self.eng.wait_ge(sem, self.n[sem.name])


def build(nc, x, ctx, mask_s, mask_c, wa, w1, w2, wm, wf, wr, er, b2, cols, rows, ident, out):
    with ExitStack() as es:
        def sb(name, shape, dt=F32):
            return es.enter_context(nc.sbuf_tensor(name, shape, dt))

        def sem(name):
            return es.enter_context(nc.semaphore(name))

        def dram(name, shape, dt):
            return nc.dram_tensor(name, shape, dt, kind="Internal").ap()

        wa_s = sb("wa_s", [P, NWA, P])
        w1_s = sb("w1_s", [P, CH0, P])
        w2_s = sb("w2_s", [P, CH0, P])
        wm_s = sb("wm_s", [P, 3, CH1, P])
        wf_s = sb("wf_s", [P, 2, CHF, P])
        wr_s = sb("wr_s", [P, 2, NEXP])
        b2_s = sb("b2_s", [NEXP, P])
        col = sb("col", [P, NCOL])
        row = sb("row", [P, NROW, P])
        idt = sb("idt", [P, P])
        er_stack = sb("er_stack", [STACK, SEQ], BF16)
        pick0 = sb("pick0", [80, NEXP, P], BF16)
        pick1 = sb("pick1", [80, NEXP // 2, P], BF16)

        X, C, N, A, B, X1 = (sb(n, [P, TILES, P]) for n in ("xs", "cs", "ns", "as_", "bs", "x1s"))
        stats = sb("stats", [P, TILES, 6])
        mv = sb("mv", [P, TILES, 2])
        var, lnv, rstd = sb("var", [P, TILES]), sb("lnv", [P, TILES]), sb("rstd", [P, TILES])
        xT, ctxT = sb("xT", [P, TOK]), sb("ctxT", [P, TOK])

        qf, kf = sb("qf", [P, TOK]), sb("kf", [P, TOK])
        q_parts, k_parts = sb("q_parts", [P, PARTS, TOK], BF16), sb("k_parts", [P, PARTS, TOK], BF16)
        q_stack, k_stack = sb("q_stack", [STACK, HEADS, TOK], BF16), sb("k_stack", [STACK, HEADS, TOK], BF16)
        er_s, er_parts = kf[0:DH, 0:SEQ], k_parts[0:DH, :, 0:SEQ]
        aT = qf
        v_aug = sb("v_aug", [P, TILES, HEADS, 32])
        g_out = sb("g_out", [P, 2, GROUP, RELW])
        rel = sb("rel", [P, 4, GROUP, RELW])
        mbias = sb("mbias", [P, 2, TILES, SEQ])
        mtop, nsc = sb("mtop", [P, 2, TILES]), sb("nsc", [P, 2, TILES])
        sc_s = sb("sc_s", [P, 3, 2 * SEQ])
        p_s = sb("p_s", [P, 3, 2 * SEQ])
        pT = sb("pT", [P, 3, 2 * SEQ])
        nmax = sb("nmax", [P, UNITS, 2])
        o_s = sb("o_s", [P, 2, TOK])
        rsum = sb("rsum", [P, TILES * GROUP])

        hid, hidw = sc_s, p_s
        lg, ex = sb("lg", [P, TILES, NEXP]), sb("ex", [P, TILES, NEXP])
        prob, sel = sb("prob", [P, TILES, NEXP]), sb("sel", [P, TILES, NEXP])
        comb = sb("comb", [P, TILES, NEXP])
        r1, r2 = sb("r1", [P, TILES]), sb("r2", [P, TILES])
        pad, padr = sb("pad", [P, TILES, 24]), sb("padr", [P, TILES, 24])
        gpad, gpadr = sb("gpad", [P, TILES, 16]), sb("gpadr", [P, TILES, 16])
        top = sb("top", [P, TILES, 8])
        ga, gb, gc, gd = (sb(n, [P, 4 * TILES]) for n in ("ga", "gb", "gc", "gd"))
        combT, comb_r = qf[0:NEXP, :], kf[0:NEXP, :]
        comb_b = sb("comb_b", [NEXP, TOK], BF16)
        comb_stack = sb("comb_stack", [80, TOK], BF16)

        bank = [es.enter_context(nc.psum_tensor(f"bank{i}", [P, 512], F32)) for i in range(8)]
        S, T, O, M = bank[0:3], bank[3:5], bank[5:7], bank[7]

        q_dram = [dram(f"q_dram{a}", (PARTS, P, TOK), BF16) for a in range(3)]
        k_dram = [dram(f"k_dram{a}", (PARTS, P, TOK), BF16) for a in range(3)]
        er_dram = dram("er_parts_dram", (PARTS, DH, SEQ), BF16)
        g0_dram = dram("g0_dram", (8, GROUP, P, P), F32)
        g1_dram = dram("g1_dram", (8, GROUP, P, SEQ), F32)

        params = sem("params")
        const = sem("const")
        er_in = sem("er_in")
        er_split, er_saved, er_loaded = sem("er_split"), sem("er_saved"), sem("er_loaded")
        go = sem("go")

        first = sem("arrive")
        arrive = first
        x_in, c_in, m_in, stored = sem("x_in"), sem("c_in"), sem("m_in"), sem("stored")
        vec, act_, pool_ = sem("vec"), sem("act_"), sem("pool_")
        var_ready, rstd_ready = sem("var_ready"), sem("rstd_ready")
        normed = sem("normed")
        turned, turn_read = sem("turned"), sem("turn_read")
        back, back_read = sem("back"), sem("back_read")
        mask_ready = sem("mask_ready")
        base_ready = sem("base_ready")
        resid = sem("resid")
        att = []
        for a in range(3):
            names = ("q_proj", "k_proj", "v_proj", "q_full", "k_full", "q_split", "k_split", "v_ready", "q_saved",
                     "k_saved", "stacked", "qk", "scored", "exped", "ptT", "pt_act", "pt_dve", "pv", "o_saved",
                     "o_turned", "o_norm", "proj")
            att.append({n: sem(f"{n}{a}") for n in names})
        g_mm, g_copied, g_saved, rel_loaded, rel_ready = (sem(n) for n in (
            "g_mm", "g_copied", "g_saved", "rel_loaded", "rel_ready"))
        logit, shifted, expd, combed, comb_turned, comb_ready = (sem(n) for n in (
            "logit", "shifted", "expd", "combed", "comb_turned", "comb_ready"))
        moe = [{n: sem(f"{n}_m{m}") for n in ("up", "y_ready", "acted", "spread", "weighted", "down")}
               for m in range(3)]
        fin = sem("fin")
        last = fin
        pass_sems = range(first.num, last.num + 1)

        PARAM_LOADS = 10

        def leave(eng, it):
            eng.sem_inc(arrive, 1)
            eng.wait_ge(go, it + 1)
            eng.wait_ge(const, 1)

        TURNS = ["ctx", "n0", "n1", "n2", "a1", "n3", "a2", "n4", "n6"]
        turn_no = {t: i + 1 for i, t in enumerate(TURNS)}
        turn_dst = {t: xT for t in TURNS} | {"ctx": ctxT, "a1": aT, "a2": aT}

        def unit(u):
            g, b, j = u // (PAIR * GROUP), u // GROUP % PAIR, u % GROUP
            return g, b, j, g * GROUP + j

        def score_cols(a, half):
            return ((0, 128), (128, 384))[half] if a == 0 else (half * SEQ, half * SEQ + SEQ)

        block = es.enter_context(nc.Block())

        @block.sync
        def _(sp):
            sp.dma_start(er_s, er).then_inc(er_in, 16)
            for dst, src in ((wa_s[:, :, :], wa), (idt[:, :], ident), (col[:, :], cols),
                             (row[:, :, :], rows), (wr_s[:, :, :], wr), (b2_s[:, :], b2), (w1_s[:, :, :], w1),
                             (w2_s[:, :, :], w2), (wf_s[:, :, :, :], wf),
                             (wm_s[:, :, :, :], wm)):
                sp.dma_start(dst, src).then_inc(params, 16)
            sp.wait_ge(er_split, 2 * PARTS - 1)
            sp.dma_start(er_dram.rearrange("j d l -> d j l"), er_parts).then_inc(er_saved, 16)
            sp.wait_ge(er_saved, 16)
            for n in range(PARTS * PARTS):
                sp.dma_start(er_stack[DH * n:DH * n + DH, :], er_dram[n // PARTS]).then_inc(er_loaded, 16)

            def stacks(a):
                s = att[a]
                sp.wait_ge(s["q_split"], 1)
                sp.dma_start(q_dram[a].rearrange("j p t -> p j t"), q_parts[:, :, :]).then_inc(s["q_saved"], 16)
                sp.wait_ge(s["k_split"], 1)
                sp.dma_start(k_dram[a].rearrange("j p t -> p j t"), k_parts[:, :, :]).then_inc(s["k_saved"], 16)
                sp.wait_ge(s["q_saved"], 16)
                q_src = q_dram[a].rearrange("j (d h) t -> (j d) h t", h=HEADS)
                for n in range(PARTS):
                    sp.dma_start(q_stack[24 * n:24 * n + 24, :, :], q_src).then_inc(s["stacked"], 16)
                sp.wait_ge(s["k_saved"], 16)
                k_src = k_dram[a].rearrange("j (d h) t -> j d h t", h=HEADS)
                for n in range(PARTS * PARTS):
                    sp.dma_start(k_stack[DH * n:DH * n + DH, :, :], k_src[n // PARTS]).then_inc(s["stacked"], 16)

            def skew(c):
                sp.wait_ge(g_copied, GROUP * (c + 1))
                sp.dma_start(g0_dram[c].rearrange("h s l -> s h l"), g_out[:, c % 2, :, 0:128]).then_inc(g_saved, 16)
                sp.dma_start(g1_dram[c].rearrange("h s l -> s h l"), g_out[:, c % 2, :, 128:384]).then_inc(g_saved, 16)
                if c >= 4:
                    sp.wait_ge(att[0]["scored"], 2 * GROUP * (c - 3))
                sp.wait_ge(g_saved, 32 * (c + 1))
                for d, w, dst in ((g0_dram, 128, rel[:, c % 4, :, 0:128]), (g1_dram, SEQ, rel[:, c % 4, :, 128:384])):
                    src = bass.AP(tensor=d.tensor, offset=c * GROUP * P * w + P - 1,
                                  ap=[[w - 1, P], [P * w, GROUP], [1, w]])
                    sp.dma_start(dst, src).then_inc(rel_loaded, 16)

            x_v = x.rearrange("(n b) (c p) d -> n p b c d", b=PAIR, p=P)
            c_v = ctx.rearrange("(n b) (c p) d -> n p b c d", b=PAIR, p=P)
            o_v = out.rearrange("(n b) (c p) d -> n p b c d", b=PAIR, p=P)
            m_v = [m.rearrange("(n b) o (c p) t -> n p b (o c) t", b=PAIR, p=P) for m in (mask_s, mask_c)]
            with sp.Fori(0, PASSES) as it:
                for b in range(PAIR):
                    sp.dma_start(X[:, 2 * b:2 * b + 2, :], x_v[it, :, b]).then_inc(x_in, 16)
                    sp.dma_start(C[:, 2 * b:2 * b + 2, :], c_v[it, :, b]).then_inc(c_in, 16)
                for m in range(2):
                    for b in range(PAIR):
                        sp.dma_start(mbias[:, m, 2 * b:2 * b + 2, :].bitcast(I32), m_v[m][it, :, b]).then_inc(m_in, 16)
                stacks(0)
                for c in range(UNITS // GROUP):
                    skew(c)
                stacks(1)
                stacks(2)
                sp.wait_ge(fin, 1)
                for b in range(PAIR):
                    sp.dma_start(o_v[it, :, b], A[:, 2 * b:2 * b + 2, :]).then_inc(stored, 16)
                sp.wait_ge(stored, 16 * PAIR)
                sp.wait_ge(arrive, 4)
                sp.sem_clear(pass_sems)
                sp.sem_inc(go, 1)

        @block.gpsimd
        def _(g):
            g.memset(pick0[:, :, :], 0.0).then_inc(const, 1)
            g.memset(pick1[:, :, :], 0.0).then_inc(const, 1)
            g.memset(comb_stack[:, :], 0.0).then_inc(const, 1)
            g.memset(v_aug[:, :, :, :], 0.0).then_inc(const, 1)
            g.memset(pad[:, :, :], -BIG).then_inc(const, 1)
            g.memset(gpad[:, :, :], -BIG).then_inc(const, 1)
            g.wait_ge(const, 6)
            g.memset(v_aug[:, :, :, DH:DH + 1], 1.0).then_inc(const, 1)
            steps = 7
            for q in range(3):
                k = slice(32 * q, 32 * q + NEXP)
                halves = pick1[k].rearrange("k c (e m) -> k c e m", e=2)
                for dst, pattern in ((pick0[k], [[-1, NEXP], [0, P]]), (halves, [[-2, NEXP // 2], [-1, 2], [0, 64]])):
                    g.wait_ge(const, steps)
                    g.affine_select(out=dst, in_=dst, compare_op=ALU.not_equal, fill=1.0, base=0, pattern=pattern,
                                    channel_multiplier=1).then_inc(const, 1)
                    steps += 1

            def split_k(a):
                s = att[a]
                g.wait_ge(s["k_full"], 2)
                t.done(g.tensor_tensor(kf[:, :], kf[:, :], k_parts[:, 0, :], ALU.subtract), pool_)
                t.settle(pool_)
                t.done(g.tensor_copy(k_parts[:, 1, :], kf[:, :]), pool_)
                t.settle(pool_)
                t.done(g.tensor_tensor(k_parts[:, 2, :], kf[:, :], k_parts[:, 1, :], ALU.subtract), s["k_split"])

            def causal(c):
                g.wait_ge(rel_loaded, 32 * (c + 1))
                for n, lo in enumerate((0, 256)):
                    v = rel[:, c % 4, :, lo:lo + P]
                    g.affine_select(out=v, in_=v, compare_op=ALU.is_ge, fill=CAUSAL, base=0,
                                    pattern=[[0, GROUP], [-1, P]], channel_multiplier=1).then_inc(rel_ready, 1)

            def base(one, two):
                t.done(g.tensor_tensor(B[:, :, :], one, two, ALU.add), base_ready)

            def spread_row(r):
                return row[:, r, :].unsqueeze(1).to_broadcast([P, TILES, P])

            with g.Fori(0, PASSES) as it:
                t = Tally(g)
                g.wait_ge(const, 13)
                split_k(0)
                for c in range(UNITS // GROUP):
                    causal(c)
                g.wait_ge(normed, 2)
                base(X1[:, :, :], N[:, :, :])
                split_k(1)
                g.wait_ge(normed, 3)
                base(N[:, :, :], spread_row(ROW_BO))
                split_k(2)
                g.wait_ge(normed, 4)
                base(N[:, :, :], spread_row(ROW_BO + 1))
                g.wait_ge(normed, 7)
                base(X1[:, :, :], N[:, :, :])
                t.settle(base_ready)
                leave(g, it)

        @block.scalar
        def _(act):
            def norm_root(k):
                act.wait_ge(var_ready, k)
                t.done(act.activation(lnv[:, :], var[:, :], ACT.Ln), act_)
                t.settle(act_)
                t.done(act.activation(rstd[:, :], lnv[:, :], ACT.Exp, scale=-0.5), rstd_ready)

            def turn(what):
                act.wait_ge(turned, turn_no[what])
                t.done(act.activation(turn_dst[what][:, :], M[:, :], ACT.Copy), turn_read)

            def project(a):
                s = att[a]
                for n, (w, full, parts, c) in enumerate((("q", qf, q_parts, COL_BQ), ("k", kf, k_parts, COL_BK))):
                    act.wait_ge(s[w + "_proj"], 1)
                    b = col[:, c + a:c + a + 1]
                    if a:
                        act.wait_ge(att[a - 1][w + "_saved"], 16)
                    t.done(act.activation(full[:, :], S[n][:, :], ACT.Identity, bias=b), s[w + "_full"])
                    t.done(act.activation(parts[:, 0, :], S[n][:, :], ACT.Identity, bias=b), s[w + "_full"])

            def g_copy(n):
                c = n // GROUP
                act.wait_ge(g_mm, n + 1)
                if c >= 2:
                    act.wait_ge(g_saved, 32 * (c - 1))
                t.done(act.activation(g_out[:, c % 2, n % GROUP, :], S[2][:, 0:RELW], ACT.Copy), g_copied)

            def attend(a):
                s = att[a]
                if a == 0:
                    for n in range(3 * GROUP):
                        g_copy(n)
                for u in range(UNITS + 2):
                    if u < UNITS:
                        if u >= 3:
                            act.wait_ge(s["ptT"], u - 2)
                        for half in range(2):
                            lo, hi = score_cols(a, half)
                            act.wait_ge(s["scored"], 2 * u + half + 1)
                            t.done(act.activation(p_s[:, u % 3, lo:hi], sc_s[:, u % 3, lo:hi], ACT.Exp,
                                                  bias=nmax[:, u, half:half + 1], scale=-1.0), s["exped"])
                        if a == 0 and u + 3 * GROUP < UNITS:
                            g_copy(u + 3 * GROUP)
                    e = u - 2
                    if e >= 0 and e % 2 == 0:
                        w = RELW if a == 0 else 2 * SEQ
                        act.wait_ge(s["ptT"], e + 1)
                        if e >= 3:
                            act.wait_ge(s["pv"], e - 2)
                        t.done(act.activation(pT[:, e % 3, 0:w], T[0][:, 0:w], ACT.Copy), s["pt_act"])

            with act.Fori(0, PASSES) as it:
                t = Tally(act)
                act.wait_ge(params, 16 * (PARAM_LOADS))
                turn("ctx")
                norm_root(1)
                turn("n0")
                project(0)
                attend(0)

                norm_root(2)
                turn("n1")
                act.wait_ge(shifted, 1)
                t.done(act.activation(ex[:, :, :], lg[:, :, :], ACT.Exp), expd)
                s = moe[0]
                for c in range(CH0):
                    act.wait_ge(s["up"], c + 1)
                    if c >= 3:
                        act.wait_ge(s["weighted"], c - 2)
                    t.done(act.activation(hid[:, c % 3, :], S[c % 3][:, :], ACT.Gelu,
                                          bias=col[:, COL_B1 + c:COL_B1 + c + 1]), s["acted"])
                act.wait_ge(s["down"], CH0)
                t.done(act.activation(aT[:, :], O[0][:, :], ACT.Copy), s["y_ready"])

                norm_root(3)
                turn("n2")
                project(1)
                attend(1)
                turn("a1")
                norm_root(4)
                turn("n3")
                project(2)
                attend(2)
                turn("a2")
                norm_root(5)
                turn("n4")
                s = moe[1]
                for c in range(CHF):
                    act.wait_ge(s["up"], c + 1)
                    dst = hid[:, c, :] if c < 3 else hidw[:, 0, :]
                    t.done(act.activation(dst, (S + T)[c][:, :], ACT.Relu,
                                          bias=col[:, COL_FB1 + c:COL_FB1 + c + 1]), s["acted"])
                act.wait_ge(s["down"], 1)
                t.done(act.activation(aT[:, :], O[0][:, :], ACT.Identity, bias=col[:, COL_FB2:COL_FB2 + 1]), s["y_ready"])
                norm_root(6)
                norm_root(7)
                turn("n6")
                act.wait_ge(logit, 2)
                t.done(act.activation(ex[:, :, :], M[:, 0:TILES * NEXP].rearrange("p (i e) -> p i e", e=NEXP),
                                      ACT.Exp, scale=-1.0), expd)
                s = moe[2]
                for c in range(CH1):
                    act.wait_ge(s["up"], c + 1)
                    if c >= 3:
                        act.wait_ge(s["weighted"], c - 2)
                    t.done(act.activation(hid[:, c % 3, :], S[c % 2][:, :], ACT.Silu), s["acted"])
                act.wait_ge(s["down"], CH1)
                t.done(act.activation(aT[:, :], O[0][:, :], ACT.Copy), s["y_ready"])
                t.settle(s["y_ready"])
                leave(act, it)

        @block.tensor
        def _(pe):
            def turn(what, src, ready, n):
                pe.wait_ge(ready, n)
                for i in range(TILES):
                    ins = pe.transpose(M[:, P * i:P * i + P], src[:, i, :], idt[:, :])
                ins.then_inc(turned, 1)
                pe.wait_ge(turn_read, turn_no[what])

            def turn_back(m):
                pe.wait_ge(moe[m]["y_ready"], 1)
                for i in range(TILES):
                    ins = pe.transpose(M[:, P * i:P * i + P], aT[:, P * i:P * i + P], idt[:, :])
                ins.then_inc(back, 1)

            def qkv(a):
                s = att[a]
                src = xT if a == 1 else ctxT
                pe.matmul(S[0][:, :], wa_s[:, W_Q[a], :], xT[:, :], start=True, stop=True).then_inc(s["q_proj"], 1)
                pe.matmul(S[1][:, :], wa_s[:, W_K[a], :], src[:, :], start=True, stop=True).then_inc(s["k_proj"], 1)
                for i in range(TILES):
                    ins = pe.matmul(S[2][:, P * i:P * i + P], src[:, P * i:P * i + P], wa_s[:, W_V[a], :],
                                    start=True, stop=True)
                ins.then_inc(s["v_proj"], 1)

            def relative(n):
                _, b, _, h = unit(n)
                pe.wait_ge(g_copied, n) if n else pe.wait_ge(att[0]["v_ready"], 1)
                for half, (lo, hi) in enumerate(((128, 256), (0, 256))):
                    q0 = b * SEQ + half * P
                    c0, c1 = score_cols(0, half)
                    ins = pe.matmul(S[2][:, c0:c1], q_stack[:, h, q0:q0 + P], er_stack[:, lo:hi],
                                    start=True, stop=True)
                ins.then_inc(g_mm, 1)

            def attend(a):
                s = att[a]
                ring = 2 if a == 0 else 3
                pe.wait_ge(s["stacked"], 16 * (PARTS + PARTS * PARTS))
                pe.wait_ge(s["q_full"], 2)
                pe.wait_ge(s["k_full"], 2)
                pe.wait_ge(s["v_ready"], 1)
                if a == 0:
                    for n in range(3 * GROUP):
                        relative(n)
                for u in range(UNITS + 7):
                    if u < UNITS:
                        _, b, _, h = unit(u)
                        if u >= ring:
                            pe.wait_ge(s["scored"], 2 * (u - ring + 1))
                        for half in range(2):
                            lo, hi = score_cols(a, half)
                            q0, k0 = b * SEQ + half * P, b * SEQ
                            ins = pe.matmul(S[u % ring][:, lo:hi], q_stack[:, h, q0:q0 + P],
                                            k_stack[:, h, k0:k0 + hi - lo], start=True, stop=True)
                        ins.then_inc(s["qk"], 1)
                        if a == 0 and u + 3 * GROUP < UNITS:
                            relative(u + 3 * GROUP)
                    r = u - 2
                    if 0 <= r < UNITS:
                        pe.wait_ge(s["exped"], 2 * (r + 1))
                        if r >= 2:
                            pe.wait_ge(s["pt_dve" if r % 2 else "pt_act"], r // 2)
                        for tc in range(2):
                            for half in range(2):
                                if a == 0 and tc > half:
                                    continue
                                lo = score_cols(a, half)[0] + P * tc
                                to = (256 if tc else P * half) if a == 0 else SEQ * tc + P * half
                                ins = pe.transpose(T[r % 2][:, to:to + P], p_s[:, r % 3, lo:lo + P], idt[:, :])
                        ins.then_inc(s["ptT"], 1)
                    v = u - 4
                    if 0 <= v < UNITS:
                        g, b, j, h = unit(v)
                        pe.wait_ge(s["pt_dve" if v % 2 else "pt_act"], v // 2 + 1)
                        if g >= 2 and v % (PAIR * GROUP) == 0:
                            pe.wait_ge(s["o_saved"], g - 1)
                        o = O[g % 2][32 * j:32 * j + 32, :]
                        s0 = b * SEQ
                        pe.matmul(o[:, s0:s0 + SEQ], v_aug[:, 2 * b, h, :], pT[:, v % 3, 0:SEQ], start=True, stop=False)
                        if a == 0:
                            ins = pe.matmul(o[:, s0 + P:s0 + SEQ], v_aug[:, 2 * b + 1, h, :], pT[:, v % 3, SEQ:RELW],
                                            start=False, stop=True)
                        else:
                            ins = pe.matmul(o[:, s0:s0 + SEQ], v_aug[:, 2 * b + 1, h, :], pT[:, v % 3, SEQ:2 * SEQ],
                                            start=False, stop=True)
                        ins.then_inc(s["pv"], 1)
                    if u >= 13 and (u - 13) % 8 == 0 or u == UNITS + 5:
                        g = (u - 13) // 8
                        pe.wait_ge(s["o_saved"], g + 1)
                        if g:
                            pe.wait_ge(s["o_norm"], g)
                        for i in range(TILES):
                            ins = pe.transpose(M[:, P * i:P * i + P], o_s[:, g % 2, P * i:P * i + P], idt[:, :])
                        ins.then_inc(s["o_turned"], 1)

            def project_out(a):
                s = att[a]
                for i in range(TILES):
                    ins = pe.matmul(S[0][:, P * i:P * i + P], aT[:, P * i:P * i + P], wa_s[:, W_O[a], :],
                                    start=True, stop=True)
                ins.then_inc(s["proj"], 1)

            def route(m, n):
                for i in range(TILES):
                    ins = pe.matmul(M[:, NEXP * i:NEXP * i + NEXP], xT[:, P * i:P * i + P], wr_s[:, m, :],
                                    start=True, stop=True)
                ins.then_inc(logit, 1)

            def turn_comb(n):
                pe.wait_ge(combed, n)
                for i in range(TILES):
                    ins = pe.transpose(M[0:NEXP, P * i:P * i + P], comb[:, i, :], idt[:, :])
                ins.then_inc(comb_turned, 1)
                pe.wait_ge(comb_ready, n)

            with pe.Fori(0, PASSES) as it:
                pe.wait_ge(params, 16 * (PARAM_LOADS))
                pe.wait_ge(const, 13)
                pe.wait_ge(er_loaded, 16 * PARTS * PARTS)
                turn("ctx", C, c_in, 16 * PAIR)
                turn("n0", N, normed, 1)
                qkv(0)
                attend(0)

                turn("n1", N, normed, 2)
                route(0, 1)
                s = moe[0]
                for c in range(CH0 + 3):
                    if c < CH0:
                        if c >= 3:
                            pe.wait_ge(s["acted"], c - 2)
                        pe.matmul(S[c % 3][:, :], w1_s[:, c, :], xT[:, :], start=True, stop=True).then_inc(s["up"], 1)
                    if c == 2:
                        turn_comb(1)
                        pe.matmul(O[0][:, :], b2_s[:, :], combT, start=True, stop=False)
                    if c >= 2 and c % 2 == 0 and (c - 2) // 2 < NEXP:
                        e = (c - 2) // 2
                        if e >= 2:
                            pe.wait_ge(s["weighted"], 2 * (e - 1))
                        pe.matmul(T[e % 2][:, :], pick0[:, e, :], comb_stack[:, :], start=True,
                                  stop=True).then_inc(s["spread"], 1)
                    d = c - 3
                    if d >= 0:
                        pe.wait_ge(s["weighted"], d + 1)
                        ins = pe.matmul(O[0][:, :], w2_s[:, d, :], hidw[:, d % 3, :], start=False, stop=d == CH0 - 1)
                        ins.then_inc(s["down"], 1)
                turn_back(0)

                turn("n2", N, normed, 3)
                qkv(1)
                attend(1)
                turn("a1", A, att[1]["o_norm"], GROUPS)
                project_out(1)
                turn("n3", N, normed, 4)
                qkv(2)
                attend(2)
                turn("a2", A, att[2]["o_norm"], GROUPS)
                project_out(2)
                turn("n4", N, normed, 5)
                s = moe[1]
                for c in range(CHF):
                    pe.matmul((S + T)[c][:, :], wf_s[:, 0, c, :], xT[:, :], start=True, stop=True).then_inc(s["up"], 1)
                for c in range(CHF):
                    pe.wait_ge(s["acted"], c + 1)
                    h = hid[:, c, :] if c < 3 else hidw[:, 0, :]
                    ins = pe.matmul(O[0][:, :], wf_s[:, 1, c, :], h, start=c == 0, stop=c == CHF - 1)
                ins.then_inc(s["down"], 1)
                turn_back(1)

                turn("n6", N, normed, 7)
                route(1, 2)
                s = moe[2]
                for c in range(CH1 + 2):
                    if c < CH1:
                        if c >= 2:
                            pe.wait_ge(s["acted"], c - 1)
                            pe.wait_ge(s["weighted"], c - 1)
                        pe.matmul([S[2], O[1]][c % 2][:, :], wm_s[:, 1, c, :], xT[:, :], start=True, stop=True)
                        pe.matmul(S[c % 2][:, :], wm_s[:, 0, c, :], xT[:, :], start=True, stop=True).then_inc(s["up"], 1)
                        if c == 1:
                            turn_comb(2)
                        if c >= 1:
                            pe.matmul(T[c % 2][:, :], pick1[:, c - 1, :], comb_stack[:, :], start=True,
                                      stop=True).then_inc(s["spread"], 1)
                    d = c - 2
                    if d >= 0:
                        pe.wait_ge(s["weighted"], d + 1)
                        ins = pe.matmul(O[0][:, :], wm_s[:, 2, d, :], hidw[:, d % 3, :], start=d == 0, stop=d == CH1 - 1)
                        ins.then_inc(s["down"], 1)
                turn_back(2)
                pe.wait_ge(back, 3)
                leave(pe, it)

        @block.vector
        def _(v):
            def serial(ins):
                t.done(ins, vec)
                t.settle(vec)

            def norm(k, src, affine=None):
                for i in range(TILES):
                    t.done(v.bn_stats(stats[:, i, :], src[:, i, :]), vec)
                t.settle(vec)
                for i in range(TILES):
                    t.done(v.bn_aggr(mv[:, i, :], stats[:, i, :]), vec)
                t.settle(vec)
                t.done(v.tensor_scalar(var[:, :], mv[:, :, 1], EPS, None, ALU.add), var_ready)
                v.wait_ge(rstd_ready, k)
                for i in range(TILES):
                    t.done(v.tensor_scalar(N[:, i, :], src[:, i, :], mv[:, i, 0:1], rstd[:, i:i + 1],
                                           ALU.subtract, ALU.mult),
                           normed if affine is None and i == TILES - 1 else vec)
                if affine is not None:
                    t.settle(vec)
                    gain, shift = (row[:, r + affine, :].unsqueeze(1).to_broadcast([P, TILES, P])
                                   for r in (ROW_G, ROW_B))
                    serial(v.tensor_tensor(N[:, :, :], N[:, :, :], gain, ALU.mult))
                    t.done(v.tensor_tensor(N[:, :, :], N[:, :, :], shift, ALU.add), normed)
                t.settle(normed)

            def split_q(a):
                s = att[a]
                v.wait_ge(s["q_full"], 2)
                serial(v.tensor_tensor(qf[:, :], qf[:, :], q_parts[:, 0, :], ALU.subtract))
                serial(v.tensor_copy(q_parts[:, 1, :], qf[:, :]))
                t.done(v.tensor_tensor(q_parts[:, 2, :], qf[:, :], q_parts[:, 1, :], ALU.subtract), s["q_split"])

            def values(a):
                s = att[a]
                v.wait_ge(s["v_proj"], 1)
                bias = row[:, ROW_BV + a, :].rearrange("p (h d) -> p h d", d=DH)
                for i in range(TILES):
                    ins = v.tensor_tensor(v_aug[:, i, :, 0:DH], S[2][:, P * i:P * i + P].rearrange("p (h d) -> p h d", d=DH),
                                          bias, ALU.add)
                    t.done(ins, vec if i < TILES - 1 else s["v_ready"])

            def attend(a):
                s = att[a]
                ring = 2 if a == 0 else 3
                for u in range(UNITS + 7):
                    if u < UNITS:
                        _, b, j, h = unit(u)
                        v.wait_ge(s["qk"], u + 1)
                        if u >= 3:
                            v.wait_ge(s["exped"], 2 * (u - 2))
                        if a == 0 and u % GROUP == 0:
                            v.wait_ge(rel_ready, 2 * (u // GROUP + 1))
                        for half in range(2):
                            lo, hi = score_cols(a, half)
                            if a == 0:
                                add, scale = rel[:, u // GROUP % 4, j, lo:hi], -SCALE
                            else:
                                i = 2 * b + half
                                add, scale = mbias[:, a - 1, i, :], nsc[:, a - 1, i:i + 1]
                            ins = v.tensor_tensor_reduce(sc_s[:, u % 3, lo:hi], S[u % ring][:, lo:hi], add, scale, BIG,
                                                         ALU.add, ALU.min, nmax[:, u, half:half + 1])
                            t.done(ins, s["scored"])
                    e = u - 2
                    if 0 <= e < UNITS and e % 2:
                        w = RELW if a == 0 else 2 * SEQ
                        v.wait_ge(s["ptT"], e + 1)
                        if e >= 3:
                            v.wait_ge(s["pv"], e - 2)
                        t.done(v.tensor_copy(pT[:, e % 3, 0:w], T[1][:, 0:w]), s["pt_dve"])
                    if u >= 12 and (u - 12) % 8 == 0:
                        g = (u - 12) // 8
                        v.wait_ge(s["pv"], 8 * (g + 1))
                        if g >= 2:
                            v.wait_ge(s["o_turned"], g - 1)
                        t.done(v.tensor_copy(o_s[:, g % 2, :], O[g % 2][:, :]), s["o_saved"])
                    if u >= 14 and (u - 14) % 8 == 0:
                        g = (u - 14) // 8
                        v.wait_ge(s["o_turned"], g + 1)
                        m = M[:, :].rearrange("p (i j c) -> p i j c", i=TILES, j=GROUP)
                        sums = M[:, :].rearrange("p (n c) -> p n c", c=32)[:, :, DH]
                        serial(v.reciprocal(rsum[:, :], sums))
                        dst = A[:, :, GROUP * DH * g:GROUP * DH * (g + 1)].rearrange("p i (j d) -> p i j d", d=DH)
                        r = rsum[:, :].rearrange("p (i j) -> p i j", j=GROUP).unsqueeze(3)
                        t.done(v.tensor_tensor(dst, m[:, :, :, 0:DH], r.to_broadcast([P, TILES, GROUP, DH]), ALU.mult),
                               s["o_norm"])
                v.wait_ge(s["o_norm"], GROUPS)

            def masks():
                v.wait_ge(m_in, 32 * PAIR)
                for m in range(2):
                    serial(v.tensor_scalar(mbias[:, m, :, :], mbias[:, m, :, :].bitcast(I32), 0.0, MASKED,
                                           ALU.is_equal, ALU.mult))
                    serial(v.tensor_reduce(mtop[:, m, :], mbias[:, m, :, :], AX.X, ALU.max))
                    serial(v.tensor_scalar(nsc[:, m, :], mtop[:, m, :], 0.0, -SCALE, ALU.is_ge, ALU.mult))

            def pick(src, dst, keep, width, choices):
                for i in range(TILES):
                    t.done(v.max(top[:, i, :], src[:, i, 0:width]), vec)
                t.settle(vec)
                serial(v.memset(top[:, :, keep:8], -BIG))
                out = padr if src is pad else gpadr
                for i in range(TILES):
                    t.done(v.match_replace(out[:, i, 0:width], top[:, i, :], src[:, i, 0:width], BIG), vec)
                t.settle(vec)
                serial(v.tensor_scalar(dst, out[:, :, 0:choices], BIG, None, ALU.is_equal))

            def over_experts(t_):
                return t_[:, :].unsqueeze(2).to_broadcast([P, TILES, NEXP])

            def route0():
                v.wait_ge(logit, 1)
                m = M[:, 0:TILES * NEXP].rearrange("p (i e) -> p i e", e=NEXP)
                bias = row[:, ROW_R, 0:NEXP].unsqueeze(1).to_broadcast([P, TILES, NEXP])
                serial(v.tensor_tensor(lg[:, :, :], m, bias, ALU.add))
                serial(v.tensor_reduce(r1[:, :], lg[:, :, :], AX.X, ALU.max))
                t.done(v.tensor_tensor(lg[:, :, :], lg[:, :, :], over_experts(r1), ALU.subtract), shifted)
                v.wait_ge(expd, 1)
                serial(v.tensor_reduce(r1[:, :], ex[:, :, :], AX.X, ALU.add))
                serial(v.reciprocal(r2[:, :], r1[:, :]))
                serial(v.tensor_tensor(pad[:, :, 0:NEXP], ex[:, :, :], over_experts(r2), ALU.mult))
                pick(pad, sel[:, :, :], 2, 24, NEXP)
                serial(v.tensor_tensor(sel[:, :, :], sel[:, :, :], pad[:, :, 0:NEXP], ALU.mult))
                serial(v.tensor_reduce(r1[:, :], sel[:, :, :], AX.X, ALU.add))
                serial(v.tensor_scalar(r1[:, :], r1[:, :], 1e-9, None, ALU.max))
                serial(v.reciprocal(r2[:, :], r1[:, :]))
                t.done(v.tensor_tensor(comb[:, :, :], sel[:, :, :], over_experts(r2), ALU.mult), combed)

            def route1():
                v.wait_ge(expd, 2)
                serial(v.tensor_scalar(ex[:, :, :], ex[:, :, :], 1.0, None, ALU.add))
                serial(v.reciprocal(prob[:, :, :], ex[:, :, :]))
                bias = row[:, ROW_R, NEXP:2 * NEXP].unsqueeze(1).to_broadcast([P, TILES, NEXP])
                serial(v.tensor_tensor(lg[:, :, :], prob[:, :, :], bias, ALU.add))
                four = lg[:, :, :].rearrange("p i (g e) -> p (i g) e", e=4)
                for dst, (one, two), op in ((ga, (0, 1), ALU.max), (gb, (0, 1), ALU.min),
                                            (gc, (2, 3), ALU.max), (gd, (2, 3), ALU.min)):
                    t.done(v.tensor_tensor(dst[:, :], four[:, :, one], four[:, :, two], op), vec)
                t.settle(vec)
                serial(v.tensor_tensor(gb[:, :], gb[:, :], gd[:, :], ALU.max))
                serial(v.tensor_tensor(gd[:, :], ga[:, :], gc[:, :], ALU.min))
                serial(v.tensor_tensor(ga[:, :], ga[:, :], gc[:, :], ALU.max))
                serial(v.tensor_tensor(gb[:, :], gb[:, :], gd[:, :], ALU.max))
                four_groups = [g_[:, :].rearrange("p (i g) -> p i g", g=4) for g_ in (ga, gb, gc)]
                serial(v.tensor_tensor(gpad[:, :, 0:4], four_groups[0], four_groups[1], ALU.add))
                pick(gpad, four_groups[2], 2, 16, 4)
                serial(v.tensor_scalar(gd[:, :], gc[:, :], -1.0, 1e30, ALU.add, ALU.mult))
                far = gd[:, :].rearrange("p (i g) -> p i g", g=4).unsqueeze(3).to_broadcast([P, TILES, 4, 4])
                serial(v.tensor_tensor(pad[:, :, 0:NEXP].rearrange("p i (g e) -> p i g e", e=4),
                                       lg[:, :, :].rearrange("p i (g e) -> p i g e", e=4), far, ALU.add))
                pick(pad, sel[:, :, :], 4, 24, NEXP)
                serial(v.tensor_tensor(sel[:, :, :], sel[:, :, :], prob[:, :, :], ALU.mult))
                serial(v.tensor_reduce(r1[:, :], sel[:, :, :], AX.X, ALU.add))
                serial(v.tensor_scalar(r1[:, :], r1[:, :], 1e-20, None, ALU.add))
                serial(v.reciprocal(r2[:, :], r1[:, :]))
                serial(v.tensor_scalar(r2[:, :], r2[:, :], 2.5, None, ALU.mult))
                t.done(v.tensor_tensor(comb[:, :, :], sel[:, :, :], over_experts(r2), ALU.mult), combed)

            def split_comb(n):
                v.wait_ge(comb_turned, n)
                serial(v.tensor_copy(combT, M[0:NEXP, :]))
                serial(v.tensor_copy(comb_stack[0:NEXP, :], combT))
                serial(v.tensor_tensor(comb_r, combT, comb_stack[0:NEXP, :], ALU.subtract))
                serial(v.tensor_copy(comb_b[:, :], comb_r))
                serial(v.tensor_copy(comb_stack[32:32 + NEXP, :], comb_b[:, :]))
                serial(v.tensor_tensor(comb_r, comb_r, comb_b[:, :], ALU.subtract))
                t.done(v.tensor_copy(comb_stack[64:64 + NEXP, :], comb_r), comb_ready)

            def rows_of(b_):
                return b_[:, :].rearrange("p (i d) -> p i d", d=P)

            def add_back(n, base, dst):
                v.wait_ge(back, n)
                t.done(v.tensor_tensor(dst[:, :, :], rows_of(M), base[:, :, :], ALU.add), back_read)
                t.settle(back_read)

            steps = 0
            v.wait_ge(er_in, 16)
            for j in range(PARTS):
                if j:
                    v.tensor_tensor(er_s, er_s, er_parts[:, j - 1, :], ALU.subtract).then_inc(er_split, 1)
                    steps += 1
                    v.wait_ge(er_split, steps)
                v.tensor_copy(er_parts[:, j, :], er_s).then_inc(er_split, 1)
                steps += 1
                v.wait_ge(er_split, steps)

            with v.Fori(0, PASSES) as it:
                t = Tally(v)
                v.wait_ge(params, 16 * (PARAM_LOADS))
                v.wait_ge(const, 13)
                v.wait_ge(x_in, 16 * PAIR)
                norm(1, X)
                split_q(0)
                values(0)
                masks()
                attend(0)
                t.done(v.tensor_tensor(X1[:, :, :], X[:, :, :], A[:, :, :], ALU.add), resid)
                t.settle(resid)
                norm(2, X1)
                route0()
                split_comb(1)
                s = moe[0]
                for c in range(CH0):
                    v.wait_ge(s["acted"], c + 1)
                    v.wait_ge(s["spread"], c // 2 + 1)
                    if c >= 3:
                        v.wait_ge(s["down"], c - 2)
                    t.done(v.tensor_tensor(hidw[:, c % 3, :], hid[:, c % 3, :], T[c // 2 % 2][:, :], ALU.mult),
                           s["weighted"])
                v.wait_ge(base_ready, 1)
                add_back(1, B, X)
                norm(3, X)
                split_q(1)
                values(1)
                attend(1)
                v.wait_ge(att[1]["proj"], 1)
                v.wait_ge(base_ready, 2)
                t.done(v.tensor_tensor(X1[:, :, :], rows_of(S[0]), B[:, :, :], ALU.add), resid)
                t.settle(resid)
                norm(4, X1, 0)
                split_q(2)
                values(2)
                attend(2)
                v.wait_ge(att[2]["proj"], 1)
                v.wait_ge(base_ready, 3)
                t.done(v.tensor_tensor(X1[:, :, :], rows_of(S[0]), B[:, :, :], ALU.add), resid)
                t.settle(resid)
                norm(5, X1, 1)
                add_back(2, N, X1)
                norm(6, X1, 2)
                t.done(v.tensor_tensor(X1[:, :, :], X[:, :, :], N[:, :, :], ALU.add), resid)
                t.settle(resid)
                norm(7, X1)
                route1()
                split_comb(2)
                s = moe[2]
                for c in range(CH1):
                    v.wait_ge(s["acted"], c + 1)
                    if c >= 3:
                        v.wait_ge(s["down"], c - 2)
                    up = [S[2], O[1]][c % 2][:, :]
                    if c == 0:
                        t.done(v.tensor_tensor(hidw[:, 0, :], hid[:, 0, :], up, ALU.mult), s["weighted"])
                    else:
                        serial(v.tensor_tensor(hid[:, c % 3, :], hid[:, c % 3, :], up, ALU.mult))
                        v.wait_ge(s["spread"], c)
                        t.done(v.tensor_tensor(hidw[:, c % 3, :], hid[:, c % 3, :], T[c % 2][:, :], ALU.mult),
                               s["weighted"])
                v.wait_ge(base_ready, 4)
                v.wait_ge(back, 3)
                t.done(v.tensor_tensor(A[:, :, :], rows_of(M), B[:, :, :], ALU.add), fin)
                t.settle(fin)
                leave(v, it)



def kernel(**inputs):
    import numpy as np
    import concourse.bacc as bacc
    from concourse.bass_utils import run_bass_kernel_spmd

    a = {k: np.asarray(v) for k, v in inputs.items()}
    order = np.arange(P).reshape(HEADS, DH).T.reshape(-1)
    l0, l1, f0, f1 = "L0_xattn_", "L1_xattn_", "L0_ffn_", "L1_ffn_"
    wa = [a[l0 + "Wq"].T[:, order], a[l0 + "Wk"].T[:, order], a[l0 + "Wv"].T]
    for n in ("sa_", "ca_"):
        wa += [a[l1 + n + "Wq"][:, order], a[l1 + n + "Wk"][:, order], a[l1 + n + "Wv"], a[l1 + n + "Wo"]]
    w1 = a[f0 + "W1"].reshape(NEXP, P, HID0 // P, P).transpose(1, 0, 2, 3).reshape(P, CH0, P)
    w2 = a[f0 + "W2"].reshape(CH0, P, P).transpose(1, 0, 2)

    def chunks(shared, routed):
        return np.concatenate([shared, routed.reshape(-1, P)]).reshape(CH1, P, P)

    wm = np.stack([chunks(a[f1 + "Ws_g"], a[f1 + "Wg"]).transpose(2, 0, 1),
                   chunks(a[f1 + "Ws_u"], a[f1 + "Wu"]).transpose(2, 0, 1),
                   chunks(a[f1 + "Ws_d"].T, a[f1 + "Wd"].transpose(0, 2, 1)).transpose(1, 0, 2)], axis=1)
    wf = np.stack([a[l1 + "ff_W1"].reshape(P, CHF, P), a[l1 + "ff_W2"].reshape(CHF, P, P).transpose(1, 0, 2)], axis=1)
    wr = np.stack([a[f0 + "Wr"], a[f1 + "gate_w"].T], axis=1)
    pre = (l0, l1 + "sa_", l1 + "ca_")
    cols = np.stack([a[p + "bq"][order] for p in pre] + [a[p + "bk"][order] for p in pre]
                    + list(a[f0 + "b1"].reshape(CH0, P)) + list(a[l1 + "ff_b1"].reshape(CHF, P)) + [a[l1 + "ff_b2"]],
                    axis=1)
    route = np.zeros(P, np.float32)
    route[0:NEXP], route[NEXP:2 * NEXP] = a[f0 + "br"], a[f1 + "gate_bias"]
    rows = np.stack([a[p + "bv"] for p in pre] + [a[l1 + "sa_bo"], a[l1 + "ca_bo"]]
                    + [a[l1 + f"ln{i}_g"] for i in (1, 2, 3)] + [a[l1 + f"ln{i}_b"] for i in (1, 2, 3)] + [route])
    rows = np.broadcast_to(rows[None], (P, NROW, P))
    arrays = {
        "x": a["x"], "ctx": a["ctx_1024"], "mask_s": a["mask_Bx1xSxS2_ik0"], "mask_c": a["mask_Bx1xSxS2_if1"],
        "wa": np.stack(wa, axis=1), "w1": w1, "w2": w2, "wm": wm, "wf": wf, "wr": wr,
        "er": a[l0 + "Er"].T, "b2": a[f0 + "b2"], "cols": cols, "rows": rows, "ident": np.eye(P, dtype=np.float32),
    }
    arrays = {k + "_in": np.ascontiguousarray(v) for k, v in arrays.items()}
    nc = bacc.Bacc("TRN2", target_bir_lowering=False, num_devices=1)
    args = [nc.dram_tensor(k, v.shape, mybir.dt.from_np(v.dtype), kind="ExternalInput").ap() for k, v in arrays.items()]
    out = nc.dram_tensor("out_dram", (BATCH, SEQ, P), F32, kind="ExternalOutput").ap()
    build(nc, *args, out)
    r = run_bass_kernel_spmd(nc, [arrays], core_ids=[0])
    return r.results[0]["out_dram"]
```

```python
from collections import defaultdict, namedtuple
from contextlib import ExitStack

import concourse.bass as bass
from concourse import mybir

F32 = mybir.dt.float32
BF16 = mybir.dt.bfloat16
I32 = mybir.dt.int32
ALU = mybir.AluOpType
ACT = mybir.ActivationFunctionType
AX = mybir.AxisListType

P = 128
BATCH, SEQ = 8, 256
PAIR = 2
PASSES = BATCH // PAIR
HALVES = SEQ // P
TILES = PAIR * HALVES
TOK = PAIR * SEQ
HEADS, DH = 16, 8
PARTS = 3
STACK = PARTS * PARTS * DH
SCALE = DH ** -0.5
MASKED = -1e9 / SCALE
CAUSAL = -1e30
EPS = 1e-5
NEXP = 16
HID0 = 256
CLUMPS = NEXP // 2
CH0 = NEXP * HID0 // P
CH1 = 1 + NEXP * 64 // P
CHF = 4
QUAD = 4
QUADS = HEADS // QUAD
VCOL = DH + 1
RELW = 384
AHEAD = 2 * QUAD
BIG = 3e38

COL_BQ, COL_BK, COL_B1, COL_FB1, COL_FB2 = 0, 3, 6, 6 + CH0, 6 + CH0 + CHF
NCOL = COL_FB2 + 1
ROW_BV, ROW_BO, ROW_G, ROW_B, ROW_R = 0, 3, 5, 8, 11
NROW = 12
W_Q, W_K, W_V, W_O = (0, 3, 7), (1, 4, 8), (2, 5, 9), (None, 6, 10)
NWA = 11

AT_VALUES, AT_COPY, AT_RESULT = 7, 7, 8
UNIT_STEPS = HEADS - QUAD + AT_RESULT + 1
M0_STEPS, M1_STEPS = 2 * CLUMPS + 2, CH1 + 3


class Tally:

    def __init__(self, eng):
        self.eng, self.n = eng, defaultdict(int)

    def done(self, ins, sem):
        ins.then_inc(sem, 1)
        self.n[sem.name] += 1

    def settle(self, sem):
        self.eng.wait_ge(sem, self.n[sem.name])


Step = namedtuple("Step", "kind b arg n run qkv rel")

LOCKS = {
    "attention": (lambda s: s[0] == "unit" and s[2][1] == 0, lambda s: s[0] == "unit" and s[2][1] == UNIT_STEPS - 1),
    "relative": (lambda s: s == ("g", s[1], 0), lambda s: s[0] == "unit" and s[2] == (0, UNIT_STEPS - 1)),
    "table": (lambda s: s[0] == "unit" and s[2][1] == 0 or s[0] == "m0" and s[2] == 0,
              lambda s: s[0] == "unit" and s[2][1] == UNIT_STEPS - 1 or s == ("y", s[1], "m0")),
    "mixture": (lambda s: s[0] == "up" or s[0] in ("m0", "m1") and s[2] == 0, lambda s: s[0] == "y"),
}


def units(a, b):
    steps = []
    for u in range(UNIT_STEPS):
        steps.append(("unit", b, (a, u)))
        if a == 0 and u + AHEAD < HEADS:
            steps.append(("g", b, u + AHEAD))
    return steps


def norm(b, what, affine=None):
    return [("stat", b, what), ("norm", b, (what, affine))]


def head(a, b):
    return [("turn", b, None), ("qkv", b, a), ("split", b, a)]


def early(b):
    return ([("load", b, None), ("ctx", b, None)] + norm(b, "X") + head(0, b) + [("mask", b, None)]
            + [("g", b, h) for h in range(AHEAD)] + units(0, b)
            + [("x1", b, "attention")] + norm(b, "X1") + [("turn", b, None), ("base", b, "X1"), ("route", b, 0),
               ("m0", b, 0), ("rank", b, (0, 0)), ("rank", b, (0, 1)), ("m0", b, 1), ("rank", b, (0, 2)),
               ("comb", b, 0), ("spread", b, 0)]
            + [("m0", b, e) for e in range(2, M0_STEPS)] + [("y", b, "m0"), ("back", b, "m0")]
            + norm(b, "X") + [("base", b, "sa")] + head(1, b) + units(1, b)
            + [("turn_a", b, None), ("out", b, 1)] + norm(b, "X1", 0))


def late(b):
    return ([("base", b, "ca")] + head(2, b) + units(2, b) + [("turn_a", b, None), ("out", b, 2)]
            + norm(b, "X1", 1) + [("turn", b, None), ("up", b, None), ("relu", b, None), ("down", b, None),
               ("y", b, "ff"), ("back", b, "ff")] + norm(b, "X1", 2) + [("x1", b, "decoder")] + norm(b, "X1")
            + [("turn", b, None), ("base", b, "X1"), ("route", b, 1), ("m1", b, 0),
               ("rank", b, (1, 0)), ("rank", b, (1, 1)), ("rank", b, (1, 2)), ("comb", b, 1), ("spread", b, 1)] + [("m1", b, c) for c in range(1, M1_STEPS)]
            + [("y", b, "m1"), ("back", b, "m1"), ("store", b, None)])


def merge(turns, *streams):
    streams = [list(s) for s in streams]
    merged, held, who = [], {}, 0
    for count in turns:
        for step in streams[who][:count]:
            for lock, (enter, leave) in LOCKS.items():
                if enter(step):
                    assert held.get(lock, who) == who, (lock, step)
                    held[lock] = who
                if leave(step):
                    held.pop(lock, None)
            merged.append(step)
        del streams[who][:count]
        who = 1 - who
    assert not any(streams)
    return merged


def number(merged):
    counter = {"ctx": "turns", "turn": "turns", "turn_a": "turns", "m0": "m0 of", "m1": "m1 of", "unit": "units of"}
    n, run, qkv, rel, out = defaultdict(int), {}, {}, {}, []
    for kind, b, arg in merged:
        c = counter.get(kind, kind)
        if kind == "unit" and arg[1] == 0:
            run[b] = n[c]
            n[c] += 1
        if kind == "g" and arg == 0:
            rel[b] = n["rel"]
            n["rel"] += 1
        if kind == "qkv":
            qkv[b] = n[c]
        if kind in ("m0", "m1"):
            if arg == 0:
                n[c] += 1
            out.append(Step(kind, b, arg, n[c] - 1, None, None, None))
            continue
        out.append(Step(kind, b, arg, n[c], run.get(b), qkv.get(b), rel.get(b)))
        if kind != "unit":
            n[c] += 1
    return out


TURNS = [
    1, 3, 2, 1, 5, 5, 1, 3, 1, 2, 1, 1, 1, 3, 1, 1, 1, 4, 1, 1, 1, 2, 1, 2, 2, 1, 1, 1, 3, 2, 2, 1, 1, 1,
    1, 2, 2, 1, 3, 2, 1, 2, 1, 2, 1, 4, 1, 1, 1, 2, 1, 1, 1, 1, 1, 1, 1, 1, 2, 4, 1, 1, 2, 3, 1, 1, 4, 1,
    3, 2, 2, 1, 2, 2, 2, 1, 2, 1, 1, 2, 2, 2, 2, 1, 2, 1, 2, 1, 2, 1, 2, 1, 1, 9, 1, 2, 1, 3, 1, 1, 1, 1,
    1, 2, 1, 10, 3, 1, 2, 1, 3, 1, 6, 1, 5, 2, 2, 6, 1, 1, 2, 2, 2, 1, 1, 1, 1, 8, 1, 5, 2, 2, 1, 1, 1, 1,
    1, 1, 5, 1, 1, 1, 11, 1, 2, 2, 1, 1, 1, 1, 2, 1, 2, 1, 1, 1, 1, 2, 2, 1, 1, 1, 1, 1, 1, 1, 6, 1, 1, 1,
    2, 1, 1, 1, 2, 1, 3, 1, 1, 1, 2, 1, 1, 1, 3, 2]


FIRST_TURNS = [
    21, 1, 13, 2, 15, 1, 4, 1, 5, 2, 2, 1, 3, 1, 2, 2, 2, 1, 2, 1, 1, 1, 1, 1, 2, 1, 2, 1, 1, 2, 1, 2, 2,
    1, 1, 10, 1, 4, 1, 9, 6, 1, 1, 1, 5, 1, 2, 1, 1, 1, 4, 1, 2, 7, 3, 1, 1, 4, 2, 1, 1, 5, 1, 6, 2, 2, 1,
    1, 2, 2, 3, 1, 1, 1, 13, 1, 2, 2, 1, 1, 1, 1, 2, 1, 2, 1, 2, 2, 2, 2, 1, 1, 2, 1, 1, 1, 1, 1, 4, 1, 3,
    2, 1, 2, 1, 1, 5, 1, 2, 1, 2, 1, 2, 1]

FIRST = number(merge(FIRST_TURNS, early(0) + late(0), early(1)))
AGAIN = number(merge(TURNS, early(0) + late(0), late(1) + early(1)))
LAST = number(late(1))
RUNS = 2 * 3


def build(nc, x, ctx, mask_s, mask_c, wa, w1, w2, wm, wf, wr, er, b2, cols, rows, ident, out):
    with ExitStack() as es:
        def sb(name, shape, dt=F32):
            return es.enter_context(nc.sbuf_tensor(name, shape, dt))

        def sem(name):
            return es.enter_context(nc.semaphore(name))

        def dram(name, shape, dt):
            return nc.dram_tensor(name, shape, dt, kind="Internal").ap()

        wa_s = sb("wa_s", [P, NWA, P])
        w1_s = sb("w1_s", [P, CH0, P])
        w2_s = sb("w2_s", [P, CH0, P])
        wm_s = sb("wm_s", [P, 3, CH1, P])
        wf_s = sb("wf_s", [P, 2, CHF, P])
        wr_s = sb("wr_s", [P, 2, NEXP])
        b2_s = sb("b2_s", [NEXP, P])
        col = sb("col", [P, NCOL])
        row = sb("row", [P, NROW, P])
        idt = sb("idt", [P, P])
        er_stack = sb("er_stack", [STACK, SEQ], BF16)
        pick0 = sb("pick0", [80, NEXP, P], BF16)
        pick1 = sb("pick1", [80, NEXP // 2, P], BF16)

        X, N, A, B, X1 = (sb(n, [P, TILES, P]) for n in ("xs", "ns", "as_", "bs", "x1s"))
        C = A
        by_name = {"X": X, "X1": X1}
        stats = sb("stats", [P, TILES, 6])
        mv = sb("mv", [P, TILES, 2])
        var, lnv, rstd = sb("var", [P, TILES]), sb("lnv", [P, TILES]), sb("rstd", [P, TILES])
        xT, ctxT = sb("xT", [P, TOK]), sb("ctxT", [P, TOK])

        qf, kf = sb("qf", [P, TOK]), sb("kf", [P, TOK])
        q_parts, k_parts = sb("q_parts", [P, PARTS, TOK], BF16), sb("k_parts", [P, PARTS, TOK], BF16)
        q_stack, k_stack = (sb(n, [STACK, PAIR, HEADS, SEQ], BF16) for n in ("q_stack", "k_stack"))
        er_s, er_parts = kf[0:DH, 0:SEQ], k_parts[0:DH, :, 0:SEQ]
        aT = qf
        v_aug = sb("v_aug", [P, TILES, HEADS, VCOL])
        g_out = sb("g_out", [P, 2, 2, RELW])
        rel = sb("rel", [P, 3, QUAD, RELW])
        mbias = sb("mbias", [P, 2, TILES, SEQ])
        mtop, nsc = sb("mtop", [P, 2, TILES]), sb("nsc", [P, 2, TILES])
        sc_s = sb("sc_s", [P, 3, 2 * SEQ])
        p_s = sb("p_s", [P, 3, 2 * SEQ])
        pT = sb("pT", [P, 2 * QUAD, 2 * SEQ])
        nmax = sb("nmax", [P, HEADS, 2])
        o_s = sb("o_s", [P, 2, SEQ])
        rsum = sb("rsum", [P, HALVES * QUAD])

        hid = sb("hid", [P, 2, 4, SEQ])
        lg, ex = sb("lg", [P, TILES, NEXP]), sb("ex", [P, TILES, NEXP])
        prob, sel = sb("prob", [P, TILES, NEXP]), sb("sel", [P, TILES, NEXP])
        comb = sb("comb", [P, TILES, NEXP])
        r1, r2 = sb("r1", [P, TILES]), sb("r2", [P, TILES])
        pad, padr = sb("pad", [P, TILES, 24]), sb("padr", [P, TILES, 24])
        gpad, gpadr = sb("gpad", [P, TILES, 16]), sb("gpadr", [P, TILES, 16])
        top = sb("top", [P, TILES, 8])
        ga, gb, gc, gd = (sb(n, [P, TILES, 4]) for n in ("ga", "gb", "gc", "gd"))
        combT, comb_r = qf[0:NEXP, :], kf[0:NEXP, :]
        comb_b = sb("comb_b", [NEXP, TOK], BF16)
        comb_stack = sb("comb_stack", [80, TOK], BF16)

        bank = [es.enter_context(nc.psum_tensor(f"bank{i}", [P, 512], F32)) for i in range(8)]
        R, O = bank[0:3], bank[3]
        H, Y, M = bank[4:6], bank[6], bank[7]

        q_dram, k_dram = (dram(n, (RUNS, PARTS, P, SEQ), BF16) for n in ("q_dram", "k_dram"))
        er_dram = dram("er_parts_dram", (PARTS, DH, SEQ), BF16)
        g0_dram = dram("g0_dram", (PAIR * HEADS, P, P), F32)
        g1_dram = dram("g1_dram", (PAIR * HEADS, P, SEQ), F32)

        params = sem("params")
        weights = sem("weights")
        const = sem("const")
        er_in = sem("er_in")
        er_split, er_saved, er_loaded = sem("er_split"), sem("er_saved"), sem("er_loaded")
        o_clear = sem("o_clear")
        go = sem("go")

        arrive = sem("arrive")
        x_in, c_in, m_in, stored = ([sem(f"{n}_{b}") for b in range(PAIR)] for n in ("x_in", "c_in", "m_in", "stored"))
        vec, act_, pool_ = sem("vec"), sem("act_"), sem("pool_")
        var_ready, rstd_ready = sem("var_ready"), sem("rstd_ready")
        normed = sem("normed")
        turned, turn_read = sem("turned"), sem("turn_read")
        y_ready = sem("y_ready")
        back, back_read = sem("back"), sem("back_read")
        base_ready = sem("base_ready")
        x1_ready = sem("x1_ready")
        qk_proj, v_proj = sem("qk_proj"), sem("v_proj")
        q_full, k_full = sem("q_full"), sem("k_full")
        q_split, k_split, v_ready = sem("q_split"), sem("k_split"), sem("v_ready")
        q_saved, k_saved = sem("q_saved"), sem("k_saved")
        q_stacked, k_stacked = ([sem(f"{n}_stacked_{run}") for run in range(RUNS)] for n in ("q", "k"))
        qk, scored, exped, ptT = sem("qk"), sem("scored"), sem("exped"), sem("ptT")
        pt_act, pt_dve, pv = sem("pt_act"), sem("pt_dve"), sem("pv")
        o_saved, o_turned, o_norm = sem("o_saved"), sem("o_turned"), sem("o_norm")
        out_proj, out_read = sem("out_proj"), sem("out_read")
        g_mm, g_copied, rel_ready = sem("g_mm"), sem("g_copied"), sem("rel_ready")
        g_saved = [sem(f"g_saved_{w}") for w in range(2)]
        rel_loaded = [sem(f"rel_loaded_{q}") for q in range(3)]
        logit, shifted, expd, combed, comb_turned, comb_read, comb_ready = (sem(n) for n in (
            "logit", "shifted", "expd", "combed", "comb_turned", "comb_read", "comb_ready"))
        moe = [{n: sem(f"{n}_m{m}") for n in ("up", "acted", "spread", "weighted", "down")} for m in range(2)]
        f_up, f_acted, f_down = sem("f_up"), sem("f_acted"), sem("f_down")
        spread_read = sem("spread_read")
        opened, gated, sigmoid = sem("opened"), sem("gated"), sem("sigmoid")
        pass_sems = range(arrive.num, sigmoid.num + 1)

        PARAM_LOADS, WEIGHT_LOADS = 6, 4
        FILLS, CONSTS = 4, 12

        def leave(eng, passes):
            eng.sem_inc(arrive, 1)
            eng.wait_ge(go, passes)
            eng.wait_ge(const, 1)

        def gate_slot(n):
            k = n % 4
            return hid[:, k // 2, 2 * (k % 2), :], hid[:, k // 2, 2 * (k % 2) + 1, :]

        def tiles(b):
            return range(HALVES * b, HALVES * b + HALVES)

        def rows_of(t_, b):
            return t_[:, HALVES * b:HALVES * (b + 1)]

        def cols_of(t_, b):
            return t_[:, SEQ * b:SEQ * (b + 1)]

        def score_bank(m):
            return R[2 * m % 3]

        def turn_bank(e):
            return R[(2 * (e + 2) + 1) % 3]

        def score_cols(a, half):
            return ((0, 128), (128, 384))[half] if a == 0 else (half * SEQ, half * SEQ + SEQ)

        block = es.enter_context(nc.Block())

        @block.sync
        def _(sp):
            sp.dma_start(er_s, er).then_inc(er_in, 16)
            for dst, src in ((idt[:, :], ident), (wa_s[:, :, :], wa), (col[:, :], cols),
                             (row[:, :, :], rows), (wr_s[:, :, :], wr), (b2_s[:, :], b2)):
                sp.dma_start(dst, src).then_inc(params, 16)

            def stack_er():
                sp.wait_ge(er_split, 2 * PARTS - 1)
                sp.dma_start(er_dram.rearrange("j d l -> d j l"), er_parts).then_inc(er_saved, 16)
                sp.wait_ge(er_saved, 16)
                for n in range(PARTS * PARTS):
                    sp.dma_start(er_stack[DH * n:DH * n + DH, :], er_dram[n // PARTS]).then_inc(er_loaded, 16)

            def save_parts(run, b, split, parts, to, saved):
                sp.wait_ge(split, run + 1)
                sp.dma_start(to[run].rearrange("j p t -> p j t"), parts[:, :, SEQ * b:SEQ * (b + 1)]).then_inc(saved, 16)

            def stack_q(run, b):
                sp.wait_ge(q_saved, 16 * (run + 1))
                src = bass.AP(tensor=q_dram.tensor, offset=run * PARTS * P * SEQ,
                              ap=[[0, PARTS], [HEADS * SEQ, PARTS * DH], [1, HEADS * SEQ]])
                sp.dma_start(q_stack[:, b], src).then_inc(q_stacked[run], 16)

            def stack_k(run, b):
                sp.wait_ge(k_saved, 16 * (run + 1))
                for j in range(PARTS):
                    src = bass.AP(tensor=k_dram.tensor, offset=(run * PARTS + j) * P * SEQ,
                                  ap=[[0, PARTS], [HEADS * SEQ, DH], [1, HEADS * SEQ]])
                    sp.dma_start(k_stack[PARTS * DH * j:PARTS * DH * (j + 1), b], src).then_inc(k_stacked[run], 16)

            def stacks(run, b, a):
                save_parts(run, b, q_split, q_parts, q_dram, q_saved)
                if a == 0:
                    stack_q(run, b)
                save_parts(run, b, k_split, k_parts, k_dram, k_saved)
                if a:
                    stack_q(run, b)
                stack_k(run, b)

            def save_g(w):
                sp.wait_ge(g_copied, 2 * (w + 1))
                for d, lo, hi in ((g0_dram, 0, 128), (g1_dram, 128, RELW)):
                    sp.dma_start(d[2 * w:2 * w + 2].rearrange("h s l -> s h l"), g_out[:, w % 2, :, lo:hi]).then_inc(g_saved[w % 2], 16)

            def load_rel(q, used):
                if q >= 3:
                    sp.wait_ge(scored, used[q - 3])
                for w in range(2):
                    sp.wait_ge(g_saved[w], 32 * (q + 1))
                for d, w, lo in ((g0_dram, 128, 0), (g1_dram, SEQ, 128)):
                    src = bass.AP(tensor=d.tensor, offset=q * QUAD * P * w + P - 1,
                                  ap=[[w - 1, P], [P * w, QUAD], [1, w]])
                    sp.dma_start(rel[:, q % 3, :, lo:lo + w], src).then_inc(rel_loaded[q % 3], 16)

            later_loads = {("load", None): [(w1_s[:, :, :], w1)], ("mask", None): [(w2_s[:, :, :], w2)],
                           ("unit", (0, HEADS - 1)): [(wf_s[:, :, :, :], wf), (wm_s[:, :, :, :], wm)]}
            x_v = x.rearrange("(n b) (c p) d -> n p b c d", b=PAIR, p=P)
            c_v = ctx.rearrange("(n b) (c p) d -> n p b c d", b=PAIR, p=P)
            o_v = out.rearrange("(n b) (c p) d -> n p b c d", b=PAIR, p=P)
            m_v = [m.rearrange("(n b) o (c p) t -> n p b (o c) t", b=PAIR, p=P) for m in (mask_s, mask_c)]

            def walk(steps, now, before):
                used, last = [], defaultdict(int)
                for kind, b, arg, n, run, _, rel_no in steps:
                    if kind == "load":
                        if last["store", b]:
                            sp.wait_ge(stored[b], 16)
                        sp.dma_start(rows_of(C, b), c_v[now, :, b]).then_inc(c_in[b], 16)
                        sp.dma_start(rows_of(X, b), x_v[now, :, b]).then_inc(x_in[b], 16)
                        for m in range(2):
                            sp.dma_start(mbias[:, m, 2 * b:2 * b + 2, :].bitcast(I32), m_v[m][now, :, b]).then_inc(m_in[b], 16)
                        if steps is FIRST and b == 0:
                            stack_er()
                    if steps is FIRST and b == 0:
                        for dst, src in later_loads.get((kind, arg), ()):
                            sp.dma_start(dst, src).then_inc(weights, 16)
                    if kind == "split":
                        stacks(n, b, arg)
                    if kind == "g" and arg % 2:
                        save_g((HEADS * rel_no + arg) // 2)
                        if arg % QUAD == QUAD - 1:
                            load_rel((HEADS * rel_no + arg) // QUAD, used)
                    if kind == "unit" and arg[0] == 0 and arg[1] < HEADS and arg[1] % QUAD == QUAD - 1:
                        used.append(2 * (HEADS * run + arg[1] + 1))
                    if kind == "store":
                        sp.wait_ge(back_read, last["back", b])
                        sp.dma_start(o_v[before if b else now, :, b], rows_of(A, b)).then_inc(stored[b], 16)
                    last[kind, b] = n + 1
                for b in range(PAIR):
                    if last["store", b]:
                        sp.wait_ge(stored[b], 16)

            def next_pass():
                sp.wait_ge(arrive, 4)
                sp.sem_clear(pass_sems)
                sp.sem_inc(go, 1)

            walk(FIRST, 0, None)
            next_pass()
            with sp.Fori(1, PASSES) as it:
                walk(AGAIN, it, it - 1)
                next_pass()
            walk(LAST, None, PASSES - 1)

        @block.gpsimd
        def _(g):
            g.memset(comb_stack[:, :], 0.0).then_inc(const, 1)
            g.memset(v_aug[:, :, :, :], 1.0).then_inc(const, 1)
            g.memset(pad[:, :, :], -BIG).then_inc(const, 1)
            g.memset(gpad[:, :, :], -BIG).then_inc(const, 1)
            g.memset(pick0[:, :, :], 0.0).then_inc(const, 1)
            g.memset(pick1[:, :, :], 0.0).then_inc(const, 1)
            steps = 6
            for q in range(3):
                k = slice(32 * q, 32 * q + NEXP)
                halves = pick1[k].rearrange("k c (e m) -> k c e m", e=2)
                for dst, pattern in ((pick0[k], [[-1, NEXP], [0, P]]), (halves, [[-2, NEXP // 2], [-1, 2], [0, 64]])):
                    g.wait_ge(const, steps)
                    g.affine_select(out=dst, in_=dst, compare_op=ALU.not_equal, fill=1.0, base=0, pattern=pattern,
                                    channel_multiplier=1).then_inc(const, 1)
                    steps += 1

            def split_k(run, b):
                g.wait_ge(k_full, 2 * (run + 1))
                f, parts = cols_of(kf, b), k_parts[:, :, SEQ * b:SEQ * (b + 1)]
                t.done(g.tensor_tensor(f, f, parts[:, 0, :], ALU.subtract), pool_)
                t.settle(pool_)
                t.done(g.tensor_copy(parts[:, 1, :], f), pool_)
                t.settle(pool_)
                t.done(g.tensor_tensor(parts[:, 2, :], f, parts[:, 1, :], ALU.subtract), k_split)

            def causal(q):
                g.wait_ge(rel_loaded[q % 3], 32 * (q // 3 + 1))
                for lo in (0, 256):
                    v = rel[:, q % 3, :, lo:lo + P]
                    g.affine_select(out=v, in_=v, compare_op=ALU.is_ge, fill=CAUSAL, base=0,
                                    pattern=[[0, QUAD], [-1, P]], channel_multiplier=1).then_inc(rel_ready, 1)

            def base(b, what, norms):
                if norms:
                    g.wait_ge(normed, norms)
                if what == "X1":
                    other = rows_of(X1, b)
                else:
                    r = ROW_BO if what == "sa" else ROW_BO + 1
                    other = row[:, r, :].unsqueeze(1).to_broadcast([P, HALVES, P])
                t.done(g.tensor_tensor(rows_of(B, b), rows_of(N, b), other, ALU.add), base_ready)

            def mixture1(order, c):
                if 2 <= c <= CH1 + 1:
                    n = CH1 * order + c - 2
                    e, h = gate_slot(n)
                    g.wait_ge(sigmoid, n + 1)
                    if c == 2:
                        g.wait_ge(gated, n + 1)
                    else:
                        g.wait_ge(spread_read, (CH1 - 1) * order + c - 2)
                    t.done(g.tensor_tensor(h, h, e, ALU.mult), moe[1]["weighted"])

            def walk(steps):
                last = defaultdict(int)
                for kind, b, arg, n, _, _, rel_no in steps:
                    if kind == "m1":
                        mixture1(n, arg)
                    if kind == "split":
                        split_k(n, b)
                    if kind == "g" and arg % QUAD == QUAD - 1:
                        causal((HEADS * rel_no + arg) // QUAD)
                    if kind == "base":
                        base(b, arg, last["norm", b])
                    last[kind, b] = n + 1
                t.settle(base_ready)

            t = Tally(g)
            g.wait_ge(const, CONSTS)
            walk(FIRST)
            leave(g, 1)
            with g.Fori(1, PASSES) as it:
                t = Tally(g)
                walk(AGAIN)
                leave(g, it + 1)
            t = Tally(g)
            walk(LAST)

        @block.scalar
        def _(act):
            table = [None]

            def exp_table():
                if table[0] != "exp":
                    act.preload_act_table_set("natural_log_exp_and_others")
                    table[0] = "exp"

            def norm_root(n, b):
                act.wait_ge(var_ready, n + 1)
                exp_table()
                t.done(act.activation(rows_of(lnv, b), rows_of(var, b), ACT.Ln), act_)
                t.settle(act_)
                t.done(act.activation(rows_of(rstd, b), rows_of(lnv, b), ACT.Exp, scale=-0.5), rstd_ready)

            def turn(n, dst):
                act.wait_ge(turned, n + 1)
                t.done(act.activation(dst, M[:, 0:SEQ], ACT.Copy), turn_read)

            def project(run, b, a):
                act.wait_ge(qk_proj, run + 1)
                for n, (full, parts, c, ready, saved) in enumerate((
                        (qf, q_parts, COL_BQ, q_full, q_saved), (kf, k_parts, COL_BK, k_full, k_saved))):
                    if run:
                        act.wait_ge(saved, 16 * run)
                    for dst in (cols_of(full, b), parts[:, 0, SEQ * b:SEQ * (b + 1)]):
                        t.done(act.activation(dst, R[0][:, SEQ * n:SEQ * (n + 1)], ACT.Identity,
                                              bias=col[:, c + a:c + a + 1]), ready)

            def copy_g(n):
                w = n // 2
                act.wait_ge(g_mm, n + 1)
                if w >= 2:
                    act.wait_ge(g_saved[w % 2], 32 * (w // 2))
                t.done(act.activation(g_out[:, w % 2, n % 2, :], M[:, 0:RELW], ACT.Copy), g_copied)

            def unit(run, b, a, u):
                m = HEADS * run + u
                e = m - 2
                if 0 <= u - 2 < HEADS and e % 2 == 0:
                    w = RELW if a == 0 else 2 * SEQ
                    act.wait_ge(ptT, e + 1)
                    if e >= 2 * QUAD:
                        act.wait_ge(pv, e // QUAD - 1)
                    t.done(act.activation(pT[:, e % 8, 0:w], turn_bank(e)[:, 0:w], ACT.Copy), pt_act)
                if u < HEADS:
                    exp_table()
                    if m >= 3:
                        act.wait_ge(ptT, m - 2)
                    for half in range(2):
                        lo, hi = score_cols(a, half)
                        act.wait_ge(scored, 2 * m + half + 1)
                        t.done(act.activation(p_s[:, m % 3, lo:hi], sc_s[:, m % 3, lo:hi], ACT.Exp,
                                              bias=nmax[:, u, half:half + 1], scale=-1.0), exped)
                if u >= AT_COPY and (u - AT_COPY) % QUAD == 0:
                    q = QUADS * run + (u - AT_COPY) // QUAD
                    act.wait_ge(pv, q + 1)
                    if q >= 2:
                        act.wait_ge(o_turned, q - 1)
                    t.done(act.activation(o_s[:, q % 2, :], O[:, 0:SEQ], ACT.Copy), o_saved)

            def mixture0(order, step):
                j, second = divmod(step, 2)
                if second and j < CLUMPS:
                    n = CLUMPS * order + j
                    act.wait_ge(moe[0]["up"], n + 1)
                    if n >= 2:
                        act.wait_ge(moe[0]["down"], n - 1)
                    for c in range(4):
                        k = COL_B1 + 4 * j + c
                        t.done(act.activation(hid[:, n % 2, c, :], H[c // 2][:, SEQ * (c % 2):SEQ * (c % 2 + 1)], ACT.Gelu,
                                              bias=col[:, k:k + 1]), moe[0]["acted"])
                    table[0] = "gelu"

            def mixture1(order, c):
                exp_table()
                if c < CH1:
                    n = CH1 * order + c
                    act.wait_ge(moe[1]["up"], n + 1)
                    if n >= 4:
                        act.wait_ge(moe[1]["down"], n - 3)
                    e, h = gate_slot(n)
                    t.done(act.activation(e, H[n % 2][:, 0:SEQ], ACT.Exp, scale=-1.0), moe[1]["acted"])
                    t.done(act.activation(h, H[n % 2][:, 0:SEQ], ACT.Copy), moe[1]["acted"])
                if 1 <= c <= CH1:
                    n = CH1 * order + c - 1
                    e = gate_slot(n)[0]
                    act.wait_ge(opened, n + 1)
                    t.done(act.activation(e, e, ACT.Ln), act_)
                    t.settle(act_)
                    t.done(act.activation(e, e, ACT.Exp, scale=-1.0), sigmoid)

            def relu(n):
                act.wait_ge(f_up, n + 1)
                for c in range(CHF):
                    t.done(act.activation(hid[:, 0, c, :], H[c // 2][:, SEQ * (c % 2):SEQ * (c % 2 + 1)], ACT.Relu,
                                          bias=col[:, COL_FB1 + c:COL_FB1 + c + 1]), f_acted)

            def take_y(b, down, count, bias=None):
                act.wait_ge(down, count)
                kind, more = (ACT.Copy, {}) if bias is None else (ACT.Identity, {"bias": bias})
                t.done(act.activation(cols_of(aT, b), Y[:, 0:SEQ], kind, **more), y_ready)

            def walk(steps):
                last, softmaxes = defaultdict(int), 0
                table[0] = None
                for kind, b, arg, n, run, _, rel_no in steps:
                    if kind == "stat":
                        norm_root(n, b)
                    if kind in ("ctx", "turn", "turn_a"):
                        turn(n, cols_of({"ctx": ctxT, "turn": xT, "turn_a": aT}[kind], b))
                    if kind == "qkv":
                        if steps is FIRST and n == 0:
                            act.wait_ge(er_saved, 16)
                        project(n, b, arg)
                    if kind == "g":
                        copy_g(HEADS * rel_no + arg)
                    if kind == "unit":
                        unit(run, b, *arg)
                    if kind == "route" and arg == 0:
                        softmaxes += 1
                        act.wait_ge(shifted, softmaxes)
                        exp_table()
                        t.done(act.activation(rows_of(ex, b), rows_of(lg, b), ACT.Exp), expd)
                    if kind == "route" and arg == 1:
                        act.wait_ge(logit, n + 1)
                        exp_table()
                        src = M[:, 0:HALVES * NEXP].rearrange("p (i e) -> p i e", e=NEXP)
                        t.done(act.activation(rows_of(ex, b), src, ACT.Exp, scale=-1.0), expd)
                    if kind == "m0":
                        mixture0(n, arg)
                    if kind == "m1":
                        mixture1(n, arg)
                    if kind == "relu":
                        relu(n)
                    if kind == "y" and arg == "m0":
                        take_y(b, moe[0]["down"], CLUMPS * last["m0", b])
                    if kind == "y" and arg == "ff":
                        take_y(b, f_down, last["down", b], col[:, COL_FB2:COL_FB2 + 1])
                    if kind == "y" and arg == "m1":
                        take_y(b, moe[1]["down"], CH1 * last["m1", b])
                    last[kind, b] = n + 1
                t.settle(y_ready)

            t = Tally(act)
            act.wait_ge(params, 16 * PARAM_LOADS)
            walk(FIRST)
            leave(act, 1)
            with act.Fori(1, PASSES) as it:
                t = Tally(act)
                walk(AGAIN)
                leave(act, it + 1)
            t = Tally(act)
            walk(LAST)

        @block.tensor
        def _(pe):
            reader = {}

            def free(which):
                if which.name in reader:
                    pe.wait_ge(*reader[which.name])

            def read_by(which, sem_, count):
                reader[which.name] = (sem_, count)

            def turn(n, src, b, ready, count):
                if count:
                    pe.wait_ge(ready, count)
                free(M)
                for i in tiles(b):
                    at = P * (i % HALVES)
                    ins = pe.transpose(M[:, at:at + P], src[:, i, :], idt[:, :])
                ins.then_inc(turned, 1)
                read_by(M, turn_read, n + 1)

            def turn_back(n, b, ys):
                pe.wait_ge(y_ready, ys)
                free(M)
                for i in tiles(b):
                    at = P * (i % HALVES)
                    ins = pe.transpose(M[:, at:at + P], aT[:, P * i:P * i + P], idt[:, :])
                ins.then_inc(back, 1)
                read_by(M, back_read, n + 1)

            def qkv(run, b, a, turns):
                src = xT if a == 1 else ctxT
                pe.wait_ge(turn_read, turns)
                free(R[1])
                for i in tiles(b):
                    at = P * (i % HALVES)
                    ins = pe.matmul(R[1][:, at:at + P], src[:, P * i:P * i + P], wa_s[:, W_V[a], :], start=True, stop=True)
                ins.then_inc(v_proj, 1)
                read_by(R[1], v_ready, run + 1)
                free(R[0])
                pe.matmul(R[0][:, 0:SEQ], wa_s[:, W_Q[a], :], cols_of(xT, b), start=True, stop=True)
                pe.matmul(R[0][:, SEQ:TOK], wa_s[:, W_K[a], :], cols_of(src, b), start=True, stop=True).then_inc(qk_proj, 1)
                read_by(R[0], k_full, 2 * (run + 1))

            def relative(n, b, h, projection):
                pe.wait_ge(q_stacked[projection], 16)
                free(M)
                for half, (lo, hi) in enumerate(((128, 256), (0, 256))):
                    c0, c1 = score_cols(0, half)
                    ins = pe.matmul(M[:, c0:c1], q_stack[:, b, h, P * half:P * (half + 1)], er_stack[:, lo:hi],
                                    start=True, stop=True)
                ins.then_inc(g_mm, 1)
                read_by(M, g_copied, n + 1)

            def unit(run, b, a, u, projection):
                m = HEADS * run + u
                if u == 0:
                    pe.wait_ge(q_stacked[projection], 16)
                    pe.wait_ge(k_stacked[projection], 16 * PARTS)
                    pe.wait_ge(v_ready, projection + 1)
                if u < HEADS:
                    bank_ = score_bank(m)
                    free(bank_)
                    for half in range(2):
                        lo, hi = score_cols(a, half)
                        ins = pe.matmul(bank_[:, lo:hi], q_stack[:, b, u, P * half:P * (half + 1)],
                                        k_stack[:, b, u, 0:hi - lo], start=True, stop=True)
                    ins.then_inc(qk, 1)
                    read_by(bank_, scored, 2 * (m + 1))
                e = m - 2
                if 0 <= u - 2 < HEADS:
                    pe.wait_ge(exped, 2 * (e + 1))
                    bank_ = turn_bank(e)
                    free(bank_)
                    for tc in range(2):
                        for half in range(2):
                            if a == 0 and tc > half:
                                continue
                            lo = score_cols(a, half)[0] + P * tc
                            to = (256 if tc else P * half) if a == 0 else SEQ * tc + P * half
                            ins = pe.transpose(bank_[:, to:to + P], p_s[:, e % 3, lo:lo + P], idt[:, :])
                    ins.then_inc(ptT, 1)
                    read_by(bank_, pt_dve if e % 2 else pt_act, e // 2 + 1)
                if u >= AT_VALUES and (u - AT_VALUES) % QUAD == 0:
                    g = (u - AT_VALUES) // QUAD
                    q = QUADS * run + g
                    pe.wait_ge(pt_act, 2 * (q + 1))
                    pe.wait_ge(pt_dve, 2 * (q + 1))
                    free(O)
                    for tc in range(2):
                        lo = P if a == 0 and tc else 0
                        for j in range(QUAD):
                            ins = pe.matmul(O[32 * j:32 * j + VCOL, lo:SEQ], v_aug[:, HALVES * b + tc, QUAD * g + j, :],
                                            pT[:, (QUAD * q + j) % 8, SEQ * tc:SEQ * tc + SEQ - lo],
                                            start=tc == 0, stop=tc == 1)
                    ins.then_inc(pv, 1)
                    read_by(O, o_saved, q + 1)
                if u >= AT_RESULT and (u - AT_RESULT) % QUAD == 0:
                    q = QUADS * run + (u - AT_RESULT) // QUAD
                    pe.wait_ge(o_saved, q + 1)
                    free(M)
                    for i in range(HALVES):
                        ins = pe.transpose(M[:, P * i:P * i + P], o_s[:, q % 2, P * i:P * i + P], idt[:, :])
                    ins.then_inc(o_turned, 1)
                    read_by(M, o_norm, q + 1)

            def project_out(n, b, a, turns):
                pe.wait_ge(turn_read, turns)
                free(R[0])
                for i in tiles(b):
                    at = P * (i % HALVES)
                    ins = pe.matmul(R[0][:, at:at + P], aT[:, P * i:P * i + P], wa_s[:, W_O[a], :], start=True, stop=True)
                ins.then_inc(out_proj, 1)
                read_by(R[0], out_read, n + 1)

            def route(n, b, m, turns):
                pe.wait_ge(turn_read, turns)
                free(M)
                for i in tiles(b):
                    at = NEXP * (i % HALVES)
                    ins = pe.matmul(M[:, at:at + NEXP], xT[:, P * i:P * i + P], wr_s[:, m, :], start=True, stop=True)
                ins.then_inc(logit, 1)
                read_by(M, expd, n + 1)

            def turn_comb(n, b, routed):
                pe.wait_ge(combed, routed)
                free(M)
                for i in tiles(b):
                    at = P * (i % HALVES)
                    ins = pe.transpose(M[0:NEXP, at:at + P], comb[:, i, :], idt[:, :])
                ins.then_inc(comb_turned, 1)
                read_by(M, comb_read, n + 1)

            def mixture0(b, order, step, combs):
                s = moe[0]
                j, second = divmod(step, 2)
                n = CLUMPS * order + j
                if not second and j:
                    if j == 1:
                        pe.wait_ge(comb_ready, combs)
                        free(Y)
                        pe.matmul(Y[:, 0:SEQ], b2_s[:, :], cols_of(combT, b), start=True, stop=False)
                    free(M)
                    for i in range(2):
                        ins = pe.matmul(M[:, SEQ * i:SEQ * (i + 1)], pick0[:, 2 * (j - 1) + i, :], cols_of(comb_stack, b),
                                        start=True, stop=True)
                    ins.then_inc(s["spread"], 1)
                    read_by(M, s["weighted"], n)
                if not second and j < CLUMPS:
                    for c in range(4):
                        if c % 2 == 0:
                            free(H[c // 2])
                        ins = pe.matmul(H[c // 2][:, SEQ * (c % 2):SEQ * (c % 2 + 1)], w1_s[:, 4 * j + c, :],
                                        cols_of(xT, b), start=True, stop=True)
                    ins.then_inc(s["up"], 1)
                    for h in range(2):
                        read_by(H[h], s["acted"], 4 * n + 2 * (h + 1))
                if second and j:
                    pe.wait_ge(s["weighted"], n)
                    for c in range(4):
                        ins = pe.matmul(Y[:, 0:SEQ], w2_s[:, 4 * (j - 1) + c, :], hid[:, (n - 1) % 2, c, :],
                                        start=False, stop=j == CLUMPS and c == 3)
                    ins.then_inc(s["down"], 1)

            def mixture1(b, order, c, combs):
                s = moe[1]
                if 2 <= c <= CH1:
                    if c == 2:
                        pe.wait_ge(comb_ready, combs)
                    free(M)
                    pe.matmul(M[:, 0:SEQ], pick1[:, c - 2, :], cols_of(comb_stack, b), start=True,
                              stop=True).then_inc(s["spread"], 1)
                    read_by(M, spread_read, (CH1 - 1) * order + c - 1)
                if c < CH1:
                    n = CH1 * order + c
                    free(H[n % 2])
                    for w in range(2):
                        ins = pe.matmul(H[n % 2][:, SEQ * w:SEQ * (w + 1)], wm_s[:, w, c, :], cols_of(xT, b),
                                        start=True, stop=True)
                    ins.then_inc(s["up"], 1)
                    read_by(H[n % 2], gated, n + 1)
                if c >= 3:
                    n = CH1 * order + c - 3
                    pe.wait_ge(s["weighted"], n + 1)
                    if c == 3:
                        free(Y)
                    pe.matmul(Y[:, 0:SEQ], wm_s[:, 2, c - 3, :], gate_slot(n)[1],
                              start=c == 3, stop=c == M1_STEPS - 1).then_inc(s["down"], 1)

            def forward_up(n, b, turns):
                pe.wait_ge(turn_read, turns)
                for c in range(CHF):
                    if c % 2 == 0:
                        free(H[c // 2])
                    ins = pe.matmul(H[c // 2][:, SEQ * (c % 2):SEQ * (c % 2 + 1)], wf_s[:, 0, c, :], cols_of(xT, b),
                                    start=True, stop=True)
                ins.then_inc(f_up, 1)
                for h in range(2):
                    read_by(H[h], f_acted, CHF * (n + 1))

            def forward_down(n):
                free(Y)
                for c in range(CHF):
                    pe.wait_ge(f_acted, CHF * n + c + 1)
                    ins = pe.matmul(Y[:, 0:SEQ], wf_s[:, 1, c, :], hid[:, 0, c, :], start=c == 0, stop=c == CHF - 1)
                ins.then_inc(f_down, 1)

            def walk(steps):
                reader.clear()
                last = defaultdict(int)
                for step in steps:
                    if steps is FIRST and step == first_mixture:
                        pe.wait_ge(weights, 16 * WEIGHT_LOADS)
                        pe.wait_ge(const, CONSTS)
                    if steps is FIRST and step == first_relative:
                        pe.wait_ge(er_loaded, 16 * PARTS * PARTS)
                    kind, b, arg, n, run, projection, rel_no = step
                    turns, combs = last["turned", b], last["spread", b]
                    if kind == "ctx":
                        turn(n, C, b, c_in[b], 16)
                    if kind == "turn":
                        turn(n, N, b, normed, last["norm", b])
                    if kind == "turn_a":
                        turn(n, A, b, o_norm, last["quads", b])
                    if kind == "qkv":
                        qkv(n, b, arg, turns)
                    if kind == "g":
                        relative(HEADS * rel_no + arg, b, arg, projection)
                    if kind == "unit":
                        unit(run, b, *arg, projection)
                        last["quads", b] = QUADS * (run + 1)
                    if kind == "out":
                        project_out(n, b, arg, turns)
                    if kind == "route":
                        route(n, b, arg, turns)
                    if kind == "comb":
                        turn_comb(n, b, last["route", b])
                    if kind == "m0":
                        mixture0(b, n, arg, combs)
                    if kind == "m1":
                        mixture1(b, n, arg, combs)
                    if kind == "up":
                        forward_up(n, b, turns)
                    if kind == "down":
                        forward_down(n)
                    if kind == "y":
                        read_by(Y, y_ready, n + 1)
                    if kind == "back":
                        turn_back(n, b, last["y", b])
                    last[kind, b] = n + 1
                    if kind in ("ctx", "turn", "turn_a"):
                        last["turned", b] = n + 1

            first_mixture = [step for step in FIRST if step.kind in ("m0", "up")][0]
            first_relative = [step for step in FIRST if step.kind == "g"][0]
            pe.wait_ge(params, 16 * PARAM_LOADS)
            pe.wait_ge(o_clear, 1)
            walk(FIRST)
            leave(pe, 1)
            with pe.Fori(1, PASSES) as it:
                walk(AGAIN)
                leave(pe, it + 1)
            walk(LAST)

        @block.vector
        def _(v):
            def serial(ins):
                t.done(ins, vec)
                t.settle(vec)

            def stat(b, src):
                for i in tiles(b):
                    t.done(v.bn_stats(stats[:, i, :], src[:, i, :]), vec)
                t.settle(vec)
                for i in tiles(b):
                    t.done(v.bn_aggr(mv[:, i, :], stats[:, i, :]), vec)
                t.settle(vec)
                t.done(v.tensor_scalar(rows_of(var, b), rows_of(mv, b)[:, :, 1], EPS, None, ALU.add), var_ready)

            def norm(b, src, affine, stats_):
                v.wait_ge(rstd_ready, stats_)
                for i in tiles(b):
                    t.done(v.tensor_scalar(N[:, i, :], src[:, i, :], mv[:, i, 0:1], rstd[:, i:i + 1],
                                           ALU.subtract, ALU.mult),
                           normed if affine is None and i % HALVES == HALVES - 1 else vec)
                if affine is not None:
                    t.settle(vec)
                    gain, shift = (row[:, r + affine, :].unsqueeze(1).to_broadcast([P, HALVES, P])
                                   for r in (ROW_G, ROW_B))
                    serial(v.tensor_tensor(rows_of(N, b), rows_of(N, b), gain, ALU.mult))
                    t.done(v.tensor_tensor(rows_of(N, b), rows_of(N, b), shift, ALU.add), normed)
                t.settle(normed)

            def split_q(run, b):
                v.wait_ge(q_full, 2 * (run + 1))
                f, parts = cols_of(qf, b), q_parts[:, :, SEQ * b:SEQ * (b + 1)]
                serial(v.tensor_tensor(f, f, parts[:, 0, :], ALU.subtract))
                serial(v.tensor_copy(parts[:, 1, :], f))
                t.done(v.tensor_tensor(parts[:, 2, :], f, parts[:, 1, :], ALU.subtract), q_split)

            def values(run, b, a):
                v.wait_ge(v_proj, run + 1)
                bias = row[:, ROW_BV + a, :].rearrange("p (h d) -> p h d", d=DH)
                for i in tiles(b):
                    at = P * (i % HALVES)
                    ins = v.tensor_tensor(v_aug[:, i, :, 0:DH], R[1][:, at:at + P].rearrange("p (h d) -> p h d", d=DH),
                                          bias, ALU.add)
                    t.done(ins, vec if i % HALVES < HALVES - 1 else v_ready)

            def unit(run, b, a, u, rel_no):
                m = HEADS * run + u
                if u < HEADS:
                    v.wait_ge(qk, m + 1)
                    if m >= 3:
                        v.wait_ge(exped, 2 * (m - 2))
                    quad = QUADS * (rel_no or 0) + u // QUAD
                    if a == 0 and u % QUAD == 0:
                        v.wait_ge(rel_ready, 2 * (quad + 1))
                    for half in range(2):
                        lo, hi = score_cols(a, half)
                        if a == 0:
                            add, scale = rel[:, quad % 3, u % QUAD, lo:hi], -SCALE
                        else:
                            i = HALVES * b + half
                            add, scale = mbias[:, a - 1, i, :], nsc[:, a - 1, i:i + 1]
                        ins = v.tensor_tensor_reduce(sc_s[:, m % 3, lo:hi], score_bank(m)[:, lo:hi], add, scale, BIG,
                                                     ALU.add, ALU.min, nmax[:, u, half:half + 1])
                        t.done(ins, scored)
                e = m - 2
                if 0 <= u - 2 < HEADS and e % 2:
                    w = RELW if a == 0 else 2 * SEQ
                    v.wait_ge(ptT, e + 1)
                    if e >= 2 * QUAD:
                        v.wait_ge(pv, e // QUAD - 1)
                    t.done(v.tensor_copy(pT[:, e % 8, 0:w], turn_bank(e)[:, 0:w]), pt_dve)
                if u >= AT_RESULT and (u - AT_RESULT) % QUAD == 0:
                    g = (u - AT_RESULT) // QUAD
                    v.wait_ge(o_turned, QUADS * run + g + 1)
                    full = M[:, 0:SEQ].rearrange("p (i j c) -> p i j c", i=HALVES, j=QUAD)
                    sums = M[:, 0:SEQ].rearrange("p (n c) -> p n c", c=32)[:, :, DH]
                    serial(v.reciprocal(rsum[:, :], sums))
                    dst = rows_of(A, b)[:, :, QUAD * DH * g:QUAD * DH * (g + 1)].rearrange("p i (j d) -> p i j d", d=DH)
                    r = rsum[:, :].rearrange("p (i j) -> p i j", j=QUAD).unsqueeze(3)
                    t.done(v.tensor_tensor(dst, full[:, :, :, 0:DH], r.to_broadcast([P, HALVES, QUAD, DH]), ALU.mult),
                           o_norm)

            def masks(b):
                v.wait_ge(m_in[b], 32)
                for m in range(2):
                    bias = rows_of(mbias[:, m, :, :], b)
                    tiles_ = slice(HALVES * b, HALVES * (b + 1))
                    serial(v.tensor_scalar(bias, bias.bitcast(I32), 0.0, MASKED, ALU.is_equal, ALU.mult))
                    serial(v.tensor_reduce(mtop[:, m, tiles_], bias, AX.X, ALU.max))
                    serial(v.tensor_scalar(nsc[:, m, tiles_], mtop[:, m, tiles_], 0.0, -SCALE, ALU.is_ge, ALU.mult))

            def pick(b, src, dst, keep, width, choices):
                for i in tiles(b):
                    t.done(v.max(top[:, i, :], src[:, i, 0:width]), vec)
                t.settle(vec)
                serial(v.memset(rows_of(top, b)[:, :, keep:8], -BIG))
                found = padr if src is pad else gpadr
                for i in tiles(b):
                    t.done(v.match_replace(found[:, i, 0:width], top[:, i, :], src[:, i, 0:width], BIG), vec)
                t.settle(vec)
                serial(v.tensor_scalar(dst, rows_of(found, b)[:, :, 0:choices], BIG, None, ALU.is_equal))

            def over_experts(t_, b):
                return rows_of(t_, b).unsqueeze(2).to_broadcast([P, HALVES, NEXP])

            def router_bias(m):
                return row[:, ROW_R, NEXP * m:NEXP * (m + 1)].unsqueeze(1).to_broadcast([P, HALVES, NEXP])

            def route0(n, b):
                lg_, ex_, pad_, sel_ = rows_of(lg, b), rows_of(ex, b), rows_of(pad, b)[:, :, 0:NEXP], rows_of(sel, b)
                one, two = rows_of(r1, b), rows_of(r2, b)
                v.wait_ge(logit, n + 1)
                m = M[:, 0:HALVES * NEXP].rearrange("p (i e) -> p i e", e=NEXP)
                serial(v.tensor_tensor(lg_, m, router_bias(0), ALU.add))
                serial(v.tensor_reduce(one, lg_, AX.X, ALU.max))
                t.done(v.tensor_tensor(lg_, lg_, over_experts(r1, b), ALU.subtract), shifted)

            def rank0(b, part, routes):
                ex_, pad_, sel_ = rows_of(ex, b), rows_of(pad, b)[:, :, 0:NEXP], rows_of(sel, b)
                one, two = rows_of(r1, b), rows_of(r2, b)
                if part == 0:
                    v.wait_ge(expd, routes)
                    serial(v.tensor_reduce(one, ex_, AX.X, ALU.add))
                    serial(v.reciprocal(two, one))
                    t.done(v.tensor_tensor(pad_, ex_, over_experts(r2, b), ALU.mult), vec)
                    return
                t.settle(vec)
                if part == 1:
                    pick(b, pad, sel_, 2, 24, NEXP)
                if part == 2:
                    serial(v.tensor_tensor(sel_, sel_, pad_, ALU.mult))
                    serial(v.tensor_reduce(one, sel_, AX.X, ALU.add))
                    serial(v.tensor_scalar(one, one, 1e-9, None, ALU.max))
                    serial(v.reciprocal(two, one))
                    t.done(v.tensor_tensor(rows_of(comb, b), sel_, over_experts(r2, b), ALU.mult), combed)

            def rank1(b, part, routes):
                lg_, ex_, pr_, sel_ = (rows_of(t_, b) for t_ in (lg, ex, prob, sel))
                a_, b_, c_, d_ = (rows_of(t_, b) for t_ in (ga, gb, gc, gd))
                one, two = rows_of(r1, b), rows_of(r2, b)
                four = lg_.rearrange("p i (g e) -> p i g e", e=4)
                if part == 0:
                    v.wait_ge(expd, routes)
                    serial(v.tensor_scalar(ex_, ex_, 1.0, None, ALU.add))
                    serial(v.reciprocal(pr_, ex_))
                    t.done(v.tensor_tensor(lg_, pr_, router_bias(1), ALU.add), vec)
                    return
                t.settle(vec)
                if part == 1:
                    groups(b, four, a_, b_, c_, d_)
                    return
                serial(v.tensor_scalar(d_, c_, -1.0, 1e30, ALU.add, ALU.mult))
                far = d_.unsqueeze(3).to_broadcast([P, HALVES, 4, 4])
                serial(v.tensor_tensor(rows_of(pad, b)[:, :, 0:NEXP].rearrange("p i (g e) -> p i g e", e=4), four, far,
                                       ALU.add))
                pick(b, pad, sel_, 4, 24, NEXP)
                serial(v.tensor_tensor(sel_, sel_, pr_, ALU.mult))
                serial(v.tensor_reduce(one, sel_, AX.X, ALU.add))
                serial(v.tensor_scalar(one, one, 1e-20, None, ALU.add))
                serial(v.reciprocal(two, one))
                serial(v.tensor_scalar(two, two, 2.5, None, ALU.mult))
                t.done(v.tensor_tensor(rows_of(comb, b), sel_, over_experts(r2, b), ALU.mult), combed)

            def groups(b, four, a_, b_, c_, d_):
                for dst, (i, j), op in ((a_, (0, 1), ALU.max), (b_, (0, 1), ALU.min),
                                        (c_, (2, 3), ALU.max), (d_, (2, 3), ALU.min)):
                    t.done(v.tensor_tensor(dst, four[:, :, :, i], four[:, :, :, j], op), vec)
                t.settle(vec)
                serial(v.tensor_tensor(b_, b_, d_, ALU.max))
                serial(v.tensor_tensor(d_, a_, c_, ALU.min))
                serial(v.tensor_tensor(a_, a_, c_, ALU.max))
                serial(v.tensor_tensor(b_, b_, d_, ALU.max))
                serial(v.tensor_tensor(rows_of(gpad, b)[:, :, 0:4], a_, b_, ALU.add))
                pick(b, gpad, c_, 2, 16, 4)

            def take_comb(n, b):
                v.wait_ge(comb_turned, n + 1)
                t.done(v.tensor_copy(cols_of(combT, b), M[0:NEXP, 0:SEQ]), comb_read)

            def split_comb(b, combs):
                cT, rT, bT, stack = (cols_of(t_, b) for t_ in (combT, comb_r, comb_b, comb_stack))
                t.settle(comb_read)
                serial(v.tensor_copy(stack[0:NEXP, :], cT))
                serial(v.tensor_tensor(rT, cT, stack[0:NEXP, :], ALU.subtract))
                serial(v.tensor_copy(bT, rT))
                serial(v.tensor_copy(stack[32:32 + NEXP, :], bT))
                serial(v.tensor_tensor(rT, rT, bT, ALU.subtract))
                t.done(v.tensor_copy(stack[64:64 + NEXP, :], rT), comb_ready)

            def mixture0(order, step):
                s = moe[0]
                if step % 2 == 0 and step:
                    n = CLUMPS * order + step // 2 - 1
                    v.wait_ge(s["acted"], 4 * (n + 1))
                    v.wait_ge(s["spread"], n + 1)
                    h = hid[:, n % 2, :, :].rearrange("p (e k) t -> p e k t", e=2)
                    weight = M[:, :].rearrange("p (e t) -> p e t", e=2).unsqueeze(2).to_broadcast([P, 2, 2, SEQ])
                    t.done(v.tensor_tensor(h, h, weight, ALU.mult), s["weighted"])

            def mixture1(order, c):
                s = moe[1]
                if 1 <= c <= CH1:
                    n = CH1 * order + c - 1
                    e, h = gate_slot(n)
                    v.wait_ge(s["acted"], 2 * (n + 1))
                    t.done(v.tensor_scalar(e, e, 1.0, BIG, ALU.add, ALU.min), opened)
                    t.done(v.tensor_tensor(h, h, H[n % 2][:, SEQ:TOK], ALU.mult), gated)
                    if c > 1:
                        k = (CH1 - 1) * order + c - 1
                        t.settle(gated)
                        v.wait_ge(s["spread"], k)
                        t.done(v.tensor_tensor(h, h, M[:, 0:SEQ], ALU.mult), spread_read)

            def as_rows(bank_):
                return bank_[:, 0:SEQ].rearrange("p (i d) -> p i d", d=P)

            def add_back(n, b, base, dst, sem_=None):
                v.wait_ge(back, n + 1)
                t.done(v.tensor_tensor(rows_of(dst, b), as_rows(M), rows_of(base, b), ALU.add), back_read)
                t.settle(back_read)

            steps = 0
            v.wait_ge(er_in, 16)
            for j in range(PARTS):
                if j:
                    v.tensor_tensor(er_s, er_s, er_parts[:, j - 1, :], ALU.subtract).then_inc(er_split, 1)
                    steps += 1
                    v.wait_ge(er_split, steps)
                v.tensor_copy(er_parts[:, j, :], er_s).then_inc(er_split, 1)
                steps += 1
                v.wait_ge(er_split, steps)
            v.memset(O[:, :], 0.0).then_inc(o_clear, 1)

            def walk(steps):
                last = defaultdict(int)
                for kind, b, arg, n, run, projection, rel_no in steps:
                    if kind == "stat":
                        if last["load", b] and not last["first", b]:
                            v.wait_ge(x_in[b], 16)
                            last["first", b] = 1
                        stat(b, by_name[arg])
                    if kind == "norm":
                        norm(b, by_name[arg[0]], arg[1], last["stat", b])
                    if kind == "qkv":
                        values(n, b, arg)
                    if kind == "split":
                        split_q(n, b)
                    if kind == "mask":
                        masks(b)
                    if kind == "unit":
                        unit(run, b, *arg, rel_no)
                    if kind == "x1":
                        other = A if arg == "attention" else N
                        if arg == "attention":
                            t.settle(o_norm)
                        t.done(v.tensor_tensor(rows_of(X1, b), rows_of(X, b), rows_of(other, b), ALU.add), x1_ready)
                        t.settle(x1_ready)
                    if kind == "route":
                        if arg == 0:
                            route0(n, b)
                    if kind == "rank":
                        (rank0, rank1)[arg[0]](b, arg[1], last["route", b])
                    if kind == "comb":
                        take_comb(n, b)
                    if kind == "spread":
                        split_comb(b, last["comb", b])
                    if kind == "m0":
                        mixture0(n, arg)
                    if kind == "m1":
                        mixture1(n, arg)
                    if kind == "back":
                        base, dst = {"m0": (B, X), "ff": (N, X1), "m1": (B, A)}[arg]
                        if base is B:
                            v.wait_ge(base_ready, last["base", b])
                        add_back(n, b, base, dst)
                    if kind == "out":
                        v.wait_ge(out_proj, n + 1)
                        v.wait_ge(base_ready, last["base", b])
                        t.done(v.tensor_tensor(rows_of(X1, b), as_rows(R[0]), rows_of(B, b), ALU.add), out_read)
                        t.settle(out_read)
                    last[kind, b] = n + 1
                t.settle(back_read)

            t = Tally(v)
            v.wait_ge(params, 16 * PARAM_LOADS)
            v.wait_ge(const, FILLS)
            walk(FIRST)
            leave(v, 1)
            with v.Fori(1, PASSES) as it:
                t = Tally(v)
                walk(AGAIN)
                leave(v, it + 1)
            t = Tally(v)
            walk(LAST)


def kernel(**inputs):
    import numpy as np
    import concourse.bacc as bacc
    from concourse.bass_utils import run_bass_kernel_spmd

    a = {k: np.asarray(v) for k, v in inputs.items()}
    order = np.arange(P).reshape(HEADS, DH).T.reshape(-1)
    l0, l1, f0, f1 = "L0_xattn_", "L1_xattn_", "L0_ffn_", "L1_ffn_"
    wa = [a[l0 + "Wq"].T[:, order], a[l0 + "Wk"].T[:, order], a[l0 + "Wv"].T]
    for n in ("sa_", "ca_"):
        wa += [a[l1 + n + "Wq"][:, order], a[l1 + n + "Wk"][:, order], a[l1 + n + "Wv"], a[l1 + n + "Wo"]]
    w1 = a[f0 + "W1"].reshape(NEXP, P, HID0 // P, P).transpose(1, 0, 2, 3).reshape(P, CH0, P)
    w2 = a[f0 + "W2"].reshape(CH0, P, P).transpose(1, 0, 2)

    def chunks(shared, routed):
        return np.concatenate([shared, routed.reshape(-1, P)]).reshape(CH1, P, P)

    wm = np.stack([chunks(a[f1 + "Ws_g"], a[f1 + "Wg"]).transpose(2, 0, 1),
                   chunks(a[f1 + "Ws_u"], a[f1 + "Wu"]).transpose(2, 0, 1),
                   chunks(a[f1 + "Ws_d"].T, a[f1 + "Wd"].transpose(0, 2, 1)).transpose(1, 0, 2)], axis=1)
    wf = np.stack([a[l1 + "ff_W1"].reshape(P, CHF, P), a[l1 + "ff_W2"].reshape(CHF, P, P).transpose(1, 0, 2)], axis=1)
    wr = np.stack([a[f0 + "Wr"], a[f1 + "gate_w"].T], axis=1)
    pre = (l0, l1 + "sa_", l1 + "ca_")
    cols = np.stack([a[p + "bq"][order] for p in pre] + [a[p + "bk"][order] for p in pre]
                    + list(a[f0 + "b1"].reshape(CH0, P)) + list(a[l1 + "ff_b1"].reshape(CHF, P)) + [a[l1 + "ff_b2"]],
                    axis=1)
    route = np.zeros(P, np.float32)
    route[0:NEXP], route[NEXP:2 * NEXP] = a[f0 + "br"], a[f1 + "gate_bias"]
    rows = np.stack([a[p + "bv"] for p in pre] + [a[l1 + "sa_bo"], a[l1 + "ca_bo"]]
                    + [a[l1 + f"ln{i}_g"] for i in (1, 2, 3)] + [a[l1 + f"ln{i}_b"] for i in (1, 2, 3)] + [route])
    rows = np.broadcast_to(rows[None], (P, NROW, P))
    arrays = {
        "x": a["x"], "ctx": a["ctx_1024"], "mask_s": a["mask_Bx1xSxS2_ik0"], "mask_c": a["mask_Bx1xSxS2_if1"],
        "wa": np.stack(wa, axis=1), "w1": w1, "w2": w2, "wm": wm, "wf": wf, "wr": wr,
        "er": a[l0 + "Er"].T, "b2": a[f0 + "b2"], "cols": cols, "rows": rows, "ident": np.eye(P, dtype=np.float32),
    }
    arrays = {k + "_in": np.ascontiguousarray(v) for k, v in arrays.items()}
    nc = bacc.Bacc("TRN2", target_bir_lowering=False, num_devices=1)
    args = [nc.dram_tensor(k, v.shape, mybir.dt.from_np(v.dtype), kind="ExternalInput").ap() for k, v in arrays.items()]
    out = nc.dram_tensor("out_dram", (BATCH, SEQ, P), F32, kind="ExternalOutput").ap()
    build(nc, *args, out)
    r = run_bass_kernel_spmd(nc, [arrays], core_ids=[0])
    return r.results[0]["out_dram"]
```
